# Optimizing a Trainium2 kernel written in Bass

```python
import numpy as np
import jax
import jax.numpy as jnp

def _softmax(x, axis=-1):
    return jax.nn.softmax(x, axis=axis)

def _gelu(x):
    return jax.nn.gelu(x, approximate=True)

def _silu(x):
    return jax.nn.silu(x)

def _sigmoid(x):
    return jax.nn.sigmoid(x)

def _layernorm(x, axis=-1, eps=1e-05):
    m = jnp.mean(x, axis=axis, keepdims=True)
    v = jnp.var(x, axis=axis, keepdims=True)
    return (x - m) / jnp.sqrt(v + eps)

def _scatter_add(tgt, idx, src, axis=0):
    return tgt.at[idx].add(src)

def _segment_sum(src, seg, n):
    return jax.ops.segment_sum(src, seg, n)
kernel_name = 'mk_sandwich_d1_jaxref_r8_fcfe86'

def setup_inputs(seed: int=0):
    np.random.seed(seed)
    _w = jnp.asarray

    def _L0_attn_setup():
        import jax, jax.numpy as jnp
        import numpy as np
        B, S, IN_DIM, D_MODEL, NUM_HEADS = (4, 256, 128, 128, 16)
        HEAD_DIM = D_MODEL // NUM_HEADS
        CAUSAL = True
        NEG = -9000000000000000.0

        def _xavier(key, shape):
            fan_out, fan_in = shape
            limit = (6.0 / (fan_in + fan_out)) ** 0.5
            return jax.random.uniform(key, shape, jnp.float32, -limit, limit)
        key = jax.random.key(seed)
        ks = jax.random.split(key, 5)
        x = jax.random.normal(ks[0], (B, S, IN_DIM), jnp.float32)
        Wq = _xavier(ks[1], (D_MODEL, IN_DIM))
        Wk = _xavier(ks[2], (D_MODEL, IN_DIM))
        Wv = _xavier(ks[3], (D_MODEL, IN_DIM))
        Wo = _xavier(ks[4], (D_MODEL, D_MODEL))
        bq = jnp.zeros((D_MODEL,), jnp.float32)
        bk = jnp.zeros((D_MODEL,), jnp.float32)
        bv = jnp.zeros((D_MODEL,), jnp.float32)
        bo = jnp.zeros((D_MODEL,), jnp.float32)
        return {'x': x, 'Wq': Wq, 'bq': bq, 'Wk': Wk, 'bk': bk, 'Wv': Wv, 'bv': bv, 'Wo': Wo, 'bo': bo}
    _L0_attn_in = _L0_attn_setup()

    def _L0_ffn_setup():
        import jax, jax.numpy as jnp
        import numpy as np
        B, N, C, H, REG = (1, 2309, 128, 16, 5)
        D = C // H
        key = jax.random.key(seed)
        k0, k1, k2, k3 = jax.random.split(key, 4)
        x = jax.random.normal(k0, (B, N, C), dtype=jnp.float32)
        g_info = jax.random.normal(k1, (12, 2, C), dtype=jnp.float32)
        W_qkv = jax.random.normal(k2, (C, 3 * C), dtype=jnp.float32) * 0.02
        W_proj = jax.random.normal(k3, (C, C), dtype=jnp.float32) * 0.02
        b_proj = jnp.zeros((C,), dtype=jnp.float32)
        return {'x': x, 'g_info': g_info, 'W_qkv': W_qkv, 'W_proj': W_proj, 'b_proj': b_proj}
    _L0_ffn_in = _L0_ffn_setup()
    _d = {'L0_attn_x': _L0_attn_in['x'], 'L0_attn_Wq': _L0_attn_in['Wq'], 'L0_attn_bq': _L0_attn_in['bq'], 'L0_attn_Wk': _L0_attn_in['Wk'], 'L0_attn_bk': _L0_attn_in['bk'], 'L0_attn_Wv': _L0_attn_in['Wv'], 'L0_attn_bv': _L0_attn_in['bv'], 'L0_attn_Wo': _L0_attn_in['Wo'], 'L0_attn_bo': _L0_attn_in['bo'], 'L0_ffn_g_info': _L0_ffn_in['g_info'], 'L0_ffn_W_qkv': _L0_ffn_in['W_qkv'], 'L0_ffn_W_proj': _L0_ffn_in['W_proj'], 'L0_ffn_b_proj': _L0_ffn_in['b_proj']}
    _x0 = _d['L0_attn_x']
    _d['L0_attn_x'] = jax.random.normal(jax.random.fold_in(jax.random.key(seed), 1), (8, 512, 128), dtype=_x0.dtype)
    del _x0
    return _d

def reference(L0_attn_x, L0_attn_Wq, L0_attn_bq, L0_attn_Wk, L0_attn_bk, L0_attn_Wv, L0_attn_bv, L0_attn_Wo, L0_attn_bo, L0_ffn_g_info, L0_ffn_W_qkv, L0_ffn_W_proj, L0_ffn_b_proj):

    def _L0_attn_ref(x, Wq, bq, Wk, bk, Wv, bv, Wo, bo):
        import jax, jax.numpy as jnp
        import numpy as np
        B, S, IN_DIM, D_MODEL, NUM_HEADS = (4, 256, 128, 128, 16)
        HEAD_DIM = D_MODEL // NUM_HEADS
        CAUSAL = True
        NEG = -9000000000000000.0

        def _xavier(key, shape):
            fan_out, fan_in = shape
            limit = (6.0 / (fan_in + fan_out)) ** 0.5
            return jax.random.uniform(key, shape, jnp.float32, -limit, limit)
        batch, seq, _ = x.shape
        q = x @ Wq.T + bq
        k = x @ Wk.T + bk
        v = x @ Wv.T + bv

        def split(t):
            return t.reshape(batch, seq, NUM_HEADS, HEAD_DIM).transpose(0, 2, 1, 3)
        q, k, v = (split(q), split(k), split(v))
        scores = jnp.einsum('bhqd,bhkd->bhqk', q, k) / jnp.sqrt(jnp.float32(HEAD_DIM))
        if CAUSAL:
            mask = jnp.tril(jnp.ones((seq, seq), bool))
            scores = jnp.where(mask, scores, jnp.float32(NEG))
        attn = jax.nn.softmax(scores, axis=-1)
        out = jnp.einsum('bhqk,bhkd->bhqd', attn, v)
        out = out.transpose(0, 2, 1, 3).reshape(batch, seq, D_MODEL)
        return out @ Wo.T + bo

    def _L0_ffn_ref(x, g_info, W_qkv, W_proj, b_proj):
        import jax, jax.numpy as jnp
        import numpy as np
        B, N, C, H, REG = (1, 2309, 128, 16, 5)
        D = C // H
        Bx, Nx, Cx = x.shape
        scale = D ** (-0.5)
        qkv = (x @ W_qkv).reshape(Bx, Nx, 3, H, D)
        q, k, v = (qkv[:, :, 0], qkv[:, :, 1], qkv[:, :, 2])
        g_layer = g_info[0].reshape(-1, H, D)
        q_g = g_layer[0]
        q_pure = q[:, REG:]
        q_n = q_pure / jnp.linalg.norm(q_pure, axis=-1, keepdims=True)
        qg_n = q_g / jnp.linalg.norm(q_g, axis=-1, keepdims=True)
        sim = (qg_n[None, None] * q_n).sum(-1).mean(-1)
        sim = (sim - sim.min()) / (sim.max() - sim.min())
        pos = sim > 0.9
        logits = jnp.einsum('bqhd,bkhd->bhqk', q * scale, k)

        def masked_attn(tok_mask):
            key_mask = jnp.concatenate([jnp.ones((Bx, REG), bool), tok_mask], axis=1)
            l = jnp.where(key_mask[:, None, None, :], logits, -jnp.inf)
            a = jax.nn.softmax(l, axis=-1)
            return jnp.einsum('bhqk,bkhd->bqhd', a, v)
        x_pos = masked_attn(pos)
        x_neg = masked_attn(~pos)
        reg_out = (x_pos[:, :REG] + x_neg[:, :REG]) * 0.5
        tok_out = jnp.where(pos[:, :, None, None], x_pos[:, REG:], x_neg[:, REG:])
        out = jnp.concatenate([reg_out, tok_out], axis=1).reshape(Bx, Nx, Cx)
        return out @ W_proj + b_proj
    x = L0_attn_x
    x = x + _layernorm(_L0_attn_ref(_layernorm(x, axis=-1), L0_attn_Wq, L0_attn_bq, L0_attn_Wk, L0_attn_bk, L0_attn_Wv, L0_attn_bv, L0_attn_Wo, L0_attn_bo), axis=-1)
    x = x + _layernorm(_L0_ffn_ref(_layernorm(x, axis=-1), L0_ffn_g_info, L0_ffn_W_qkv, L0_ffn_W_proj, L0_ffn_b_proj), axis=-1)
    return x

_drawn_inputs = setup_inputs


def setup_inputs(seed=0):
    import zlib

    import numpy as np

    out = dict(_drawn_inputs(seed))
    spreads = {'L0_attn_bq': (0.0, 0.1),
     'L0_attn_bk': (0.0, 0.1),
     'L0_attn_bv': (0.0, 0.1),
     'L0_attn_bo': (0.0, 0.1),
     'L0_ffn_b_proj': (0.0, 0.1)}
    factors = {}
    for name, (base, spread) in spreads.items():
        noise = np.random.default_rng([zlib.crc32(name.encode()), seed]).standard_normal(out[name].shape)
        drawn = base * np.exp(spread * noise) if base else spread * noise
        out[name] = jnp.asarray(drawn.astype(out[name].dtype))
    for name, factor in factors.items():
        out[name] = (out[name] * factor).astype(out[name].dtype)
    return out
```

```python
from contextlib import ExitStack

import concourse.bass as bass
from concourse import mybir

F32 = mybir.dt.float32
BF16 = mybir.dt.bfloat16
U32 = mybir.dt.uint32
ALU = mybir.AluOpType
ACT = mybir.ActivationFunctionType
AX = mybir.AxisListType

B, S, D, H, HD = 8, 512, 128, 16, 8
REG = 5
NB = S // 128
PAIRS, QUADS = H // 2, H // 4
TERMS = 6
MASK_ROW = 2 * TERMS * HD
MAX_ROW = MASK_ROW + 2
ROWS = MAX_ROW + 3
VW = 32
SCALE = 1.0 / float(HD) ** 0.5
BIG = 1.0e30
EPS = 1e-5
XQ = H * REG
STEPS = 2 * QUADS
TURNS = B // 2
START = 16
Q_TERMS = (0, 1, 0, 1, 1, 2)
K_TERMS = (0, 1, 1, 0, 2, 1)


class Steps:

    def __init__(self, eng, sem, base=0):
        self.eng, self.sem, self.base, self.n = eng, sem, base, 0

    def done(self, ins):
        ins.then_inc(self.sem, 1)
        self.n += 1

    def settle(self):
        self.eng.wait_ge(self.sem, self.base + self.n)


def score_uses(causal):
    if not causal:
        return [(i, [g], S) for i in range(NB) for g in range(4)]
    return ([(3, [g], 512) for g in range(4)] + [(2, [g], 384) for g in range(4)]
            + [(1, [0, 1], 256), (1, [2, 3], 256), (0, [0, 1, 2, 3], 128)])


def exp_uses(causal, kb):
    if not causal or kb == 0:
        return [([0, 1], 512, 512), ([2, 3], 512, 512)]
    if kb == 1:
        return [([0, 1], 384, 512), ([2, 3], 384, 512)]
    if kb == 2:
        return [([0, 1, 2, 3], 256, 256)]
    return [([0, 1, 2, 3], 128, 128)]


def build(nc, x, wqT, wkT, wvT, woT, bq, bk, bv, bo, g_info, w2q, w2k, w2v, wpT, bp, ident, tri, bd_rows, bd_cols, sel_r,
          out):
    with ExitStack() as ctx:
        def sb(name, shape, dt=F32):
            return ctx.enter_context(nc.sbuf_tensor(name, shape, dt))

        def sem(name):
            return ctx.enter_context(nc.semaphore(name))

        def dram(name, shape, dt):
            return nc.dram_tensor(name, shape, dt).ap()

        x_all = sb("x_all", [128, B, NB, D])
        v_all = sb("v_all", [128, B, NB, D])
        o_all = sb("o_all", [128, B, NB, D])
        qpad = sb("qpad", [128, 2, QUADS, 4, S], BF16)
        kk = sb("kk", [128, 2, PAIRS * S], BF16)
        vpad = sb("vpad", [128, 2, NB, H, VW])
        E = sb("E", [128, 4, 4, S])
        id32 = sb("id32", [128, 128])
        id16 = sb("id16", [128, 128], BF16)
        tri_sb = sb("tri_sb", [128, 128], BF16)
        wq_sb = sb("wq_sb", [128, D])
        wk_sb = sb("wk_sb", [128, D])
        wqv_sb = sb("wqv_sb", [128, 2 * D])
        wo_sb = sb("wo_sb", [128, D])
        bq_sb = sb("bq_sb", [128, 1])
        bk_sb = sb("bk_sb", [128, 1])
        bv_bc = sb("bv_bc", [128, D])
        bo_bc = sb("bo_bc", [128, D])
        w2q_sb = sb("w2q_sb", [128, D])
        w2k_sb = sb("w2k_sb", [128, D])
        w2v_sb = sb("w2v_sb", [128, 2 * D])
        wp_sb = sb("wp_sb", [128, D])
        bp_bc = sb("bp_bc", [128, D])
        g_bc = sb("g_bc", [128, D])
        g_n = sb("g_n", [128, H])
        mhalf = sb("mhalf", [128, NB * H])
        bd_r = sb("bd_r", [128, H, REG])
        bd_c = sb("bd_c", [XQ, D])
        selr_sb = sb("selr_sb", [XQ, REG])
        sim = sb("sim", [128, B, NB])
        sx_all = E[0:XQ, 0:2].rearrange("p a g (o s) -> p (a g o) s", o=1)
        o_neg = sb("o_neg", [REG, B, D])
        o_cur = sb("o_cur", [128, NB, D])
        xn = sb("xn", [128, NB, D])
        xT = sb("xT", [128, S])
        qf = sb("qf", [128, S])
        kf = sb("kf", [128, S])
        res = sb("res", [128, S])
        parts = sb("parts", [128, 2, 3, S], BF16)
        stats = sb("stats", [128, NB, 6])
        mv = sb("mv", [128, NB, 2])
        rstd = sb("rstd", [128, NB])
        y_sb = sb("y_sb", [128, NB, D])
        oT2 = sb("oT2", [128, S])
        qtok = sb("qtok", [128, NB * D])
        prod = sb("prod", [128, NB * D])
        dots = sb("dots", [128, NB * H])
        nrm2 = sb("nrm2", [128, NB * H])
        qbd = sb("qbd", [128, H, REG])
        nm = sb("nm", [128, 2, NB, 4])
        nmr = sb("nmr", [128, 2, NB, 4])
        nms = sb("nms", [128, 2, NB, 12], BF16)
        mT = sb("mT", [12, 2, S], BF16)
        oT = sb("oT", [128, 2, S])
        rec = sb("rec", [128, NB, 4])

        work = ctx.enter_context(nc.psum_tensor("work", [128, 3, 512], F32))
        st = ctx.enter_context(nc.psum_tensor("st", [128, 2, 1024], F32))
        pv = ctx.enter_context(nc.psum_tensor("pv", [128, 512], F32))

        q_scr = dram("q_scr", [B, 2, TERMS, 64, S], BF16)
        k_scr = dram("k_scr", [B, 2, TERMS, 64, S], BF16)
        m_scr = dram("m_scr", [5, B, S], BF16)

        batch_signals = ("oT_psum oT_read o_cur_ready y_psum y_read xn_ready xT_psum xT_ready qk_psum tok_psum qk_read "
                 "tok_read split split_step stored dve_step pow_done qbd_ready sx_psum sx_read ")
        attention_signals = ("s_ready max_done split split_step mT_psum mT_ready max_row0 max_row1 qk_load0 qk_load1 v_ready0 "
                 "v_ready1 st_ready exp_done tri_done pv_done pv_read oT_psum o_done rec_done ")
        signal = {tag + name: sem(tag + name) for tags, names in (("a_ c_ f_", batch_signals), ("b_ e_", attention_signals))
                  for tag in tags.split() for name in names.split()}

        loaded = sem("loaded")
        held = sem("held")
        cleared, halves, v_zero, k_ones = sem("cleared"), sem("halves"), sem("v_zero"), sem("k_ones")
        g_step, g_pow = sem("g_step"), sem("g_pow")
        with nc.Block() as block:
            @block.sync
            def _(sp):
                loads = [(wq_sb[:], wqT), (wk_sb[:], wkT), (wqv_sb[:, 0:D], wvT), (wo_sb[:], woT),
                         (bq_sb[:], bq), (bk_sb[:], bk),
                         (bv_bc[:], bv.to_broadcast([128, D])), (bo_bc[:], bo.to_broadcast([128, D])),
                         (w2q_sb[:], w2q[:, D:2 * D]), (w2k_sb[:], w2k), (w2v_sb[:, 0:D], w2v), (w2v_sb[:, D:2 * D], w2q[:, 0:D]),
                         (wp_sb[:], wpT), (bp_bc[:], bp.to_broadcast([128, D])),
                         (g_bc[:], g_info.to_broadcast([128, D])),
                         (id32[:], ident), (tri_sb[:], tri), (bd_r[:].rearrange("p h r -> p (h r)"), bd_rows),
                         (bd_c[:], bd_cols), (selr_sb[:], sel_r)]
                loads += [(x_all[:, b, :, :], x[b].rearrange("(j p) d -> p j d", p=128)) for b in range(B)]
                for dst, src in loads:
                    sp.dma_start(dst, src).then_inc(loaded, 16)
                for s in signal.values():
                    sp.sem_inc(s, START)
                sp.wait_ge(loaded, 16 * len(loads))

            @block.vector
            def _(dve):
                nc.vector.memset(qpad[:].bitcast(U32), 0).then_inc(cleared, 1)
                steps = Steps(dve, g_step)
                n_loads = 20 + B
                dve.wait_ge(loaded, 16 * n_loads)
                nc.vector.tensor_copy(id16[:], id32[:]).then_inc(cleared, 1)
                steps.done(nc.vector.tensor_tensor(prod[:, 0:D], g_bc[:], g_bc[:], ALU.mult))
                steps.settle()
                steps.done(nc.vector.tensor_reduce(g_n[:], prod[:, 0:D].rearrange("p (h d) -> p h d", d=HD),
                                                   AX.X, ALU.add))
                steps.settle()
                dve.wait_ge(g_pow, 1)
                g3 = g_bc[:].rearrange("p (h d) -> p h d", d=HD)
                steps.done(nc.vector.tensor_tensor(g3, g3, g_n[:].unsqueeze(2).to_broadcast([128, H, HD]), ALU.mult))

            @block.gpsimd
            def _(pool):
                nc.gpsimd.memset(kk[MASK_ROW:ROWS], 1.0).then_inc(k_ones, 1)
                pool.wait_ge(k_ones, 1)
                nc.gpsimd.memset(mhalf[:], -0.5).then_inc(halves, 1)
                nc.gpsimd.memset(vpad[:], 0.0).then_inc(v_zero, 1)
                pool.wait_ge(v_zero, 1)
                nc.gpsimd.memset(vpad[:, :, :, :, HD:HD + 1].rearrange("p a k h o -> p (a k h) o"), 1.0).then_inc(cleared, 1)
                pool.wait_ge(halves, 1)
                pool.wait_ge(g_step, 2)
                nc.gpsimd.tensor_tensor(g_n[:], g_n[:], mhalf[:, 0:H], ALU.pow).then_inc(g_pow, 1)

        def apart(eng):
            eng.sem_inc(held, 1)

        def layer_norm(steps, src, dst, pow_done, nth):
            apart(steps.eng)
            for j in range(NB):
                steps.done(nc.vector.bn_stats(stats[:, j, :], src(j)))
            steps.settle()
            apart(steps.eng)
            for j in range(NB):
                steps.done(nc.vector.bn_aggr(mv[:, j, :], stats[:, j, :]))
            steps.settle()
            steps.done(nc.vector.tensor_scalar(rstd[:], mv[:, :, 1], EPS, None, ALU.add))
            steps.eng.wait_ge(pow_done, START + nth)
            for j in range(NB):
                steps.done(nc.vector.tensor_scalar(dst[:, j, :], src(j), mv[:, j, 0:1], rstd[:, j:j + 1],
                                                   ALU.subtract, ALU.mult))
            steps.settle()

        def batch_stage(tag, post, prep):
            two = prep == 2
            oT_psum, oT_read = signal[tag + "oT_psum"], signal[tag + "oT_read"]
            o_cur_ready = signal[tag + "o_cur_ready"]
            y_psum, y_read = signal[tag + "y_psum"], signal[tag + "y_read"]
            xn_ready, xT_psum, xT_ready = signal[tag + "xn_ready"], signal[tag + "xT_psum"], signal[tag + "xT_ready"]
            qk_psum, tok_psum = signal[tag + "qk_psum"], signal[tag + "tok_psum"]
            qk_read, tok_read = signal[tag + "qk_read"], signal[tag + "tok_read"]
            split, split_step, stored = signal[tag + "split"], signal[tag + "split_step"], signal[tag + "stored"]
            dve_step, pow_done = signal[tag + "dve_step"], signal[tag + "pow_done"]
            qbd_ready, sx_psum, sx_read = signal[tag + "qbd_ready"], signal[tag + "sx_psum"], signal[tag + "sx_read"]
            ps_oT, ps_y = work[:, 0, :], work[:, 1, :]
            ps_xT = work[:, 2, :]
            ps_q, ps_k = st[:, 0, 0:512], st[:, 0, 512:1024]
            ps_tok = st[:, 1, :]
            ps_sx = pv[0:XQ, :]
            wq_, wk_, wv_ = (w2q_sb, w2k_sb, w2v_sb) if two else (wq_sb, wk_sb, wqv_sb)
            TW = 2 * D if two else D

            PER = (1 + 13 if post else 0) + (12 if prep else 0) + (1 + 6 if two else 0)
            POWS = (1 if post else 0) + (1 if prep else 0) + (1 if two else 0)
            AT_POST, AT_PREP, AT_SIM = 1 + 9, (1 + 13 if post else 0) + 9, PER - 2

            with nc.Block() as block:
                @block.tensor
                def _(pe):
                    with pe.Fori(0, B) as b:
                        if post:
                            pe.wait_ge(oT_read, START + b)
                            pe.wait_ge(o_cur_ready, START + b + 1)
                            for j in range(NB):
                                mm = nc.tensor.transpose(ps_oT[:, j * 128:(j + 1) * 128], o_cur[:, j, :], id32[:])
                            mm.then_inc(oT_psum, 1)
                            pe.wait_ge(oT_read, START + b + 1)
                            pe.wait_ge(y_read, START + b)
                            for j in range(NB):
                                mm = nc.tensor.matmul(ps_y[:, j * 128:(j + 1) * 128], oT2[:, j * 128:(j + 1) * 128],
                                                      post[0][:], start=True, stop=True)
                            mm.then_inc(y_psum, 1)
                        if prep:
                            pe.wait_ge(xn_ready, START + b + 1)
                            pe.wait_ge(xT_ready, START + b)
                            for j in range(NB):
                                mm = nc.tensor.transpose(ps_xT[:, j * 128:(j + 1) * 128], xn[:, j, :], id32[:])
                            mm.then_inc(xT_psum, 1)
                            pe.wait_ge(xT_ready, START + b + 1)
                            pe.wait_ge(qk_read, START + 2 * b)
                            nc.tensor.matmul(ps_q, wq_[:], xT[:], start=True, stop=True).then_inc(qk_psum, 1)
                            nc.tensor.matmul(ps_k, wk_[:], xT[:], start=True, stop=True).then_inc(qk_psum, 1)
                            pe.wait_ge(tok_read, START + b)
                            for j in range(NB):
                                mm = nc.tensor.matmul(ps_tok[:, j * TW:(j + 1) * TW], xT[:, j * 128:(j + 1) * 128],
                                                      wv_[:, 0:TW], start=True, stop=True)
                            mm.then_inc(tok_psum, 1)
                        if two:
                            pe.wait_ge(qbd_ready, START + b + 1)
                            pe.wait_ge(qk_read, START + 2 * b + 2)
                            pe.wait_ge(sx_read, START + b)
                            nc.tensor.matmul(ps_sx, qbd[:].rearrange("p h r -> p (h r)"), kf[:],
                                             start=True, stop=True).then_inc(sx_psum, 1)

                @block.scalar
                def _(act):
                    with act.Fori(0, B) as b:
                        if post:
                            act.wait_ge(oT_psum, START + b + 1)
                            act.wait_ge(y_psum, START + b)
                            nc.scalar.copy(oT2[:], ps_oT).then_inc(oT_read, 1)
                        if prep:
                            act.wait_ge(xT_psum, START + b + 1)
                            act.wait_ge(tok_psum, START + b)
                            nc.scalar.copy(xT[:], ps_xT).then_inc(xT_ready, 1)
                            act.wait_ge(split, START + 2 * b)
                            if two:
                                act.wait_ge(sx_psum, START + b)
                            act.wait_ge(qk_psum, START + 2 * b + 1)
                            if two:
                                nc.scalar.copy(qf[:], ps_q).then_inc(qk_read, 1)
                            else:
                                nc.scalar.activation(qf[:], ps_q, ACT.Identity, bias=bq_sb[:]).then_inc(qk_read, 1)
                            act.wait_ge(qk_psum, START + 2 * b + 2)
                            if two:
                                nc.scalar.copy(kf[:], ps_k).then_inc(qk_read, 1)
                            else:
                                nc.scalar.activation(kf[:], ps_k, ACT.Identity, bias=bk_sb[:]).then_inc(qk_read, 1)
                        if two:
                            act.wait_ge(sx_psum, START + b + 1)
                            nc.scalar.copy(sx_all[:, b, :], ps_sx).then_inc(sx_read, 1)


                @block.vector
                def _(dve):
                    with dve.Fori(0, B) as b:
                        steps = Steps(dve, dve_step, START + b * PER)
                        if post:
                            dve.wait_ge(y_psum, START + b + 1)
                            y3 = ps_y.rearrange("p (j d) -> p j d", d=D)
                            ins = nc.vector.tensor_tensor(y_sb[:], y3, post[1][:].unsqueeze(1).to_broadcast([128, NB, D]),
                                                          ALU.add)
                            steps.done(ins)
                            steps.settle()
                            layer_norm(steps, lambda j: y_sb[:, j, :], y_sb, pow_done, POWS * b + 1)
                            nc.vector.tensor_tensor(x_all[:, b, :, :], x_all[:, b, :, :], y_sb[:],
                                                    ALU.add).then_inc(y_read, 1)
                            dve.wait_ge(y_read, START + b + 1)
                        if prep:
                            dve.wait_ge(xT_psum, START + b)
                            apart(dve)
                            for j in range(NB):
                                steps.done(nc.vector.bn_stats(stats[:, j, :], x_all[:, b, j, :]))
                            steps.settle()
                            apart(dve)
                            for j in range(NB):
                                steps.done(nc.vector.bn_aggr(mv[:, j, :], stats[:, j, :]))
                            steps.settle()
                            steps.done(nc.vector.tensor_scalar(rstd[:], mv[:, :, 1], EPS, None, ALU.add))
                            dve.wait_ge(pow_done, START + POWS * b + (2 if post else 1))
                            for j in range(NB):
                                ins = nc.vector.tensor_scalar(xn[:, j, :], x_all[:, b, j, :], mv[:, j, 0:1],
                                                              rstd[:, j:j + 1], ALU.subtract, ALU.mult)
                                if j < NB - 1:
                                    steps.done(ins)
                            ins.then_inc(xn_ready, 1)
                            dve.wait_ge(tok_psum, START + b + 1)
                            t3 = ps_tok[:, 0:NB * TW].rearrange("p (j w) -> p j w", w=TW)
                            if two:
                                steps.done(nc.vector.tensor_copy(v_all[:, b, :, :], t3[:, :, 0:D]))
                                nc.vector.tensor_copy(qtok[:].rearrange("p (j d) -> p j d", d=D),
                                                      t3[:, :, D:2 * D]).then_inc(tok_read, 1)
                            else:
                                nc.vector.tensor_tensor(v_all[:, b, :, :], t3, bv_bc[:].unsqueeze(1).to_broadcast([128, NB, D]),
                                                        ALU.add).then_inc(tok_read, 1)
                        if two:
                            dve.wait_ge(qk_read, START + 2 * b + 1)
                            dve.wait_ge(sx_psum, START + b)
                            nc.vector.tensor_tensor(qbd[:], bd_r[:], qf[:, 0:REG].unsqueeze(1).to_broadcast([128, H, REG]),
                                                    ALU.mult).then_inc(qbd_ready, 1)
                            dve.wait_ge(tok_read, START + b + 1)
                            q3 = qtok[:].rearrange("p (j d) -> p j d", d=D)
                            steps.done(nc.vector.tensor_tensor(prod[:].rearrange("p (j d) -> p j d", d=D), q3,
                                                               g_bc[:].unsqueeze(1).to_broadcast([128, NB, D]), ALU.mult))
                            steps.settle()
                            steps.done(nc.vector.tensor_reduce(dots[:], prod[:].rearrange("p (a d) -> p a d", d=HD),
                                                               AX.X, ALU.add))
                            steps.settle()
                            steps.done(nc.vector.tensor_tensor(prod[:], qtok[:], qtok[:], ALU.mult))
                            steps.settle()
                            steps.done(nc.vector.tensor_reduce(nrm2[:], prod[:].rearrange("p (a d) -> p a d", d=HD),
                                                               AX.X, ALU.add))
                            steps.settle()
                            dve.wait_ge(pow_done, START + POWS * b + 3)
                            steps.done(nc.vector.tensor_tensor(dots[:], dots[:], nrm2[:], ALU.mult))
                            steps.settle()
                            steps.done(nc.vector.tensor_reduce(sim[:, b, :], dots[:].rearrange("p (j h) -> p j h", h=H),
                                                               AX.X, ALU.add))
                            steps.settle()
                        n = steps.n
                        assert n == PER, n

                @block.gpsimd
                def _(pool):
                    with pool.Fori(0, B) as b:
                        if post:
                            pool.wait_ge(oT_psum, START + b)
                            apart(pool)
                            nc.gpsimd.tensor_copy(o_cur[:], o_all[:, b, :, :]).then_inc(o_cur_ready, 1)
                            pool.wait_ge(dve_step, START + b * PER + AT_POST)
                            nc.gpsimd.tensor_tensor(rstd[:], rstd[:], mhalf[:, 0:NB], ALU.pow).then_inc(pow_done, 1)
                        if prep:
                            pool.wait_ge(dve_step, START + b * PER + AT_PREP)
                            nc.gpsimd.tensor_tensor(rstd[:], rstd[:], mhalf[:, 0:NB], ALU.pow).then_inc(pow_done, 1)
                        if prep:
                            for s, src in ((0, qf), (1, kf)):
                                steps = Steps(pool, split_step, START + b * 6 + 3 * s)
                                pool.wait_ge(qk_read, START + 2 * b + 1 + s)
                                if s == 0:
                                    pool.wait_ge(stored, START + 16 * 2 * TERMS * b)
                                apart(pool)
                                steps.done(nc.gpsimd.tensor_copy(parts[:, s, 1, :], src[:]))
                                steps.settle()
                                steps.done(nc.gpsimd.tensor_tensor(res[:], src[:], parts[:, s, 1, :], ALU.subtract))
                                steps.settle()
                                apart(pool)
                                steps.done(nc.gpsimd.tensor_copy(parts[:, s, 0, :], res[:]))
                                steps.settle()
                                nc.gpsimd.tensor_tensor(parts[:, s, 2, :], res[:], parts[:, s, 0, :],
                                                        ALU.subtract).then_inc(split, 1)
                                pool.wait_ge(split, START + 2 * b + s + 1)
                        if two:
                            pool.wait_ge(dve_step, START + b * PER + AT_SIM)
                            nc.gpsimd.tensor_tensor(nrm2[:], nrm2[:], mhalf[:], ALU.pow).then_inc(pow_done, 1)

                @block.sync
                def _(sp):
                    with sp.Fori(0, B) as b:
                        if prep:
                            for s, (terms, scr) in enumerate(((Q_TERMS, q_scr), (K_TERMS, k_scr))):
                                sp.wait_ge(split, START + 2 * b + s + 1)
                                for t, part in enumerate(terms):
                                    sp.dma_start(scr[b, :, t, :, :], parts[:, s, part, :]).then_inc(stored, 16)
                        else:
                            sp.wait_ge(y_read, START + b + 1)
                            sp.dma_start(out[b].rearrange("(j p) d -> p j d", p=128), x_all[:, b, :, :]).then_inc(stored, 16)
                    sp.wait_ge(stored, START + 16 * B * (2 * TERMS if prep else 1))

        def attention_stage(tag, causal):
            uses = score_uses(causal)
            NS = len(uses)
            NE = sum(len(exp_uses(causal, kb)) for kb in range(NB))
            n_loads = 3 if causal else 5
            quarters = [uses[len(uses) * t // 4:len(uses) * (t + 1) // 4] for t in range(4)]
            s_ready, max_done = signal[tag + "s_ready"], signal[tag + "max_done"]
            split, split_step = signal[tag + "split"], signal[tag + "split_step"]
            mT_psum, mT_ready = signal[tag + "mT_psum"], signal[tag + "mT_ready"]
            max_row = [signal[tag + "max_row0"], signal[tag + "max_row1"]]
            qk_load = [signal[tag + "qk_load0"], signal[tag + "qk_load1"]]
            v_ready = [signal[tag + "v_ready0"], signal[tag + "v_ready1"]]
            st_ready, exp_done, tri_done = signal[tag + "st_ready"], signal[tag + "exp_done"], signal[tag + "tri_done"]
            pv_done, pv_read = signal[tag + "pv_done"], signal[tag + "pv_read"]
            oT_psum, o_done, rec_done = signal[tag + "oT_psum"], signal[tag + "o_done"], signal[tag + "rec_done"]

            def ring_banks(NS, where):
                if where == "prologue":
                    return (2 * NS) % 3
                n, at = 0, {}
                for m in range(STEPS):
                    for kb in range(NB):
                        if not (where == "last" and m + 2 >= STEPS):
                            for t in range(len(quarters[kb])):
                                at[("s", m, kb, t)] = n % 3
                                n += 1
                        if kb == 1 and not (where == "last" and m + 1 == STEPS):
                            at[("mT", m + 1)] = n % 3
                            n += 1
                        if kb == 2 and m > 0:
                            at[("o", m - 1)] = n % 3
                            n += 1
                at[("o", STEPS - 1)] = n % 3
                return at

            def last_and_turns(eng, body):
                with eng.Fori(0, TURNS - 1) as turn:
                    body(turn, False)
                body(TURNS - 1, True)

            with nc.Block() as block:
                @block.tensor
                def _(pe):
                    slot_wait = [None] * 3
                    ring = [0]

                    def take(sem_, value):
                        w = ring[0] % 3
                        ring[0] += 1
                        if slot_wait[w]:
                            pe.wait_ge(slot_wait[w][0], START + slot_wait[w][1])
                        slot_wait[w] = (sem_, value)
                        return work[:, w, :]

                    def first_scores(par, c, quarter, base):
                        before = sum(len(quarters[t]) for t in range(quarter))
                        for n, (i, heads, keys) in enumerate(quarters[quarter]):
                            bank = take(max_done, base + before + n + 1)
                            for k, g in enumerate(heads):
                                p = 2 * c + g % 2
                                o = bank[:, k * keys:(k + 1) * keys]
                                mm = nc.tensor.matmul(o, qpad[0:MAX_ROW, par, c, g, i * 128:(i + 1) * 128],
                                                      kk[0:MAX_ROW, par, p * S:p * S + keys], start=True, stop=not causal)
                                if causal:
                                    mm = nc.tensor.matmul(o[:, keys - 128:keys], id16[:], tri_sb[:], start=False, stop=True)
                            mm.then_inc(s_ready, 1)

                    def max_transpose(slot, nth):
                        bank = take(mT_ready, nth + 1).bitcast(BF16)
                        pe.wait_ge(split, START + nth + 1)
                        for i in range(NB):
                            mm = nc.tensor.transpose(bank[0:12, i * 128:(i + 1) * 128], nms[:, slot, i, :], id16[:])
                        mm.then_inc(mT_psum, 1)

                    def second_scores(turn, m, kb, k):
                        par, c = m // 4, m % 4
                        if kb == 0:
                            pe.wait_ge(max_row[m % 2], START + 16 * (4 * turn + m // 2 + 1))
                        for heads, queries, stride in exp_uses(causal, kb):
                            pe.wait_ge(exp_done, START + turn * STEPS * NE + max(k - 1, 0))
                            for a, g in enumerate(heads):
                                p = 2 * c + g % 2
                                mm = nc.tensor.matmul(st[:, k % 2, a * stride:a * stride + queries],
                                                      kk[0:ROWS, par, p * S + kb * 128:p * S + (kb + 1) * 128],
                                                      qpad[0:ROWS, par, c, g, S - queries:S],
                                                      start=True, stop=True)
                            mm.then_inc(st_ready, 1)
                            k += 1
                        return k

                    def weigh_values(turn, m, kb, exps):
                        par, c = m // 4, m % 4
                        u = 4 * m + kb
                        if kb == 0:
                            pe.wait_ge(pv_read, START + turn * STEPS + m)
                            if c == 0:
                                pe.wait_ge(v_ready[par], START + turn + 1)
                        if causal:
                            pe.wait_ge(tri_done, START + turn * 4 * STEPS + u + 1)
                        pe.wait_ge(exp_done, START + turn * STEPS * NE + exps)
                        lo = kb * 128 if causal else 0
                        for g in range(4):
                            mm = nc.tensor.matmul(pv[32 * g:32 * g + VW, lo:S], vpad[:, par, kb, 4 * c + g, :],
                                                  E[:, u % 4, g, 0:S - lo], start=(kb == 0), stop=(kb == NB - 1),
                                                  tile_position=(0, 32 * g), skip_group_check=True)
                        mm.then_inc(pv_done, 1)

                    def out_transpose(turn, m):
                        bank = take(o_done, turn * STEPS + m + 1)
                        pe.wait_ge(pv_read, START + turn * STEPS + m + 1)
                        for i in range(NB):
                            mm = nc.tensor.transpose(bank[:, i * 128:(i + 1) * 128], oT[:, m % 2, i * 128:(i + 1) * 128],
                                                     id32[:])
                        mm.then_inc(oT_psum, 1)

                    pe.wait_ge(qk_load[0], START + 16 * n_loads)
                    for c in range(2):
                        for t in range(4):
                            first_scores(0, c, t, c * NS)
                    max_transpose(0, 0)

                    def body(turn, last):
                        pe.wait_ge(max_done, START + 2 * NS + turn * STEPS * NS)
                        pe.wait_ge(mT_ready, START + 1 + turn * STEPS)
                        pe.wait_ge(o_done, START + turn * STEPS)
                        slot_wait[:] = [None] * 3
                        ring[0] = 0
                        k, exps = 0, {}
                        for m in range(STEPS):
                            ahead = (m + 2) % STEPS
                            for kb in range(NB):
                                k = second_scores(turn, m, kb, k)
                                exps[4 * m + kb] = k
                                if not (last and m + 2 >= STEPS):
                                    if kb == 0 and m == 2:
                                        pe.wait_ge(qk_load[1], START + 16 * n_loads * (turn + 1))
                                    if kb == 0 and m == 6:
                                        pe.wait_ge(qk_load[0], START + 16 * n_loads * (turn + 2))
                                    first_scores(ahead // 4, ahead % 4, kb, 2 * NS + (turn * STEPS + m) * NS)
                                u = 4 * m + kb - 1
                                if u >= 0:
                                    weigh_values(turn, u // 4, u % 4, exps[u])
                                if kb == 1 and not (last and m + 1 == STEPS):
                                    max_transpose((m + 1) % 2, turn * STEPS + m + 1)
                                if kb == 2 and m > 0:
                                    out_transpose(turn, m - 1)
                        weigh_values(turn, STEPS - 1, NB - 1, exps[4 * STEPS - 1])
                        out_transpose(turn, STEPS - 1)

                    last_and_turns(pe, body)

                @block.scalar
                def _(act):
                    def max_read(slot, nth, half):
                        act.wait_ge(mT_psum, START + nth + 1)
                        act.wait_ge(max_row[slot], START + 16 * half)
                        bank = work[:, mt_bank[0], :].bitcast(BF16)
                        nc.scalar.copy(mT[:, slot, :], bank[0:12, 0:512]).then_inc(mT_ready, 1)

                    def pv_evac(turn, m):
                        act.wait_ge(pv_done, START + turn * 4 * STEPS + 4 * m + 4)
                        if m >= 2:
                            act.wait_ge(oT_psum, START + turn * STEPS + m - 1)
                        else:
                            act.wait_ge(oT_psum, START + turn * STEPS)
                        nc.scalar.copy(oT[:, m % 2, :], pv[:]).then_inc(pv_read, 1)

                    mt_bank = [ring_banks(NS, "prologue")]
                    max_read(0, 0, 0)

                    def body(turn, last):
                        banks = ring_banks(NS, "last" if last else "turn")
                        k = 0
                        for m in range(STEPS):
                            for kb in range(NB):
                                u = 4 * m + kb
                                for a, (heads, queries, stride) in enumerate(exp_uses(causal, kb)):
                                    act.wait_ge(st_ready, START + turn * STEPS * NE + k + 1)
                                    if a == 0:
                                        act.wait_ge(pv_done, START + turn * 4 * STEPS + max(u - 3, 0))
                                    src = st[:, k % 2, 0:stride * len(heads)].rearrange("p (h q) -> p h q", q=stride)
                                    nc.scalar.activation(E[:, u % 4, heads[0]:heads[-1] + 1, 0:queries],
                                                         src[:, :, 0:queries], ACT.Exp, scale=SCALE).then_inc(exp_done, 1)
                                    k += 1
                                if kb == 0 and m > 0:
                                    pv_evac(turn, m - 1)
                                if kb == 1 and not (last and m + 1 == STEPS):
                                    mt_bank[0] = banks[("mT", m + 1)]
                                    max_read((m + 1) % 2, turn * STEPS + m + 1, 4 * turn + (m + 1) // 2)
                        pv_evac(turn, STEPS - 1)

                    last_and_turns(act, body)

                @block.vector
                def _(dve):
                    def row_max(w, slot, use, base):
                        i, heads, keys = use
                        dve.wait_ge(s_ready, START + base + 1)
                        src = work[:, w, 0:keys * len(heads)].rearrange("p (h k) -> p h k", k=keys)
                        nc.vector.tensor_reduce(nm[:, slot, i, heads[0]:heads[-1] + 1], src, AX.X, ALU.max,
                                                negate=True).then_inc(max_done, 1)

                    def normalise(turn, m, w):
                        c = m % 4
                        o4 = work[:, w, :].rearrange("p (i g r) -> p i g r", i=NB, g=4)
                        dve.wait_ge(oT_psum, START + turn * STEPS + m + 1)
                        dve.wait_ge(o_done, START + turn * STEPS + m)
                        nc.vector.reciprocal(rec[:], o4[:, :, :, HD]).then_inc(rec_done, 1)
                        dve.wait_ge(rec_done, START + turn * STEPS + m + 1)
                        dst = o_all[:, 2 * turn + m // 4, :, 4 * HD * c:4 * HD * (c + 1)].rearrange("p i (g d) -> p i g d", d=HD)
                        nc.vector.tensor_tensor(dst, o4[:, :, :, 0:HD], rec[:].unsqueeze(3).to_broadcast([128, NB, 4, HD]),
                                                ALU.mult).then_inc(o_done, 1)

                    w = 0
                    for c in range(2):
                        for n, use in enumerate(uses):
                            row_max(w % 3, c, use, c * NS + n)
                            w += 1

                    def body(turn, last):
                        banks = ring_banks(NS, "last" if last else "turn")
                        for m in range(STEPS):
                            for kb in range(NB):
                                if not (last and m + 2 >= STEPS):
                                    if kb == 0:
                                        dve.wait_ge(split, START + turn * STEPS + m + 1)
                                    before = sum(len(quarters[t]) for t in range(kb))
                                    for n, use in enumerate(quarters[kb]):
                                        row_max(banks[("s", m, kb, n)], m % 2, use,
                                                2 * NS + (turn * STEPS + m) * NS + before + n)
                                if kb == 2 and m > 0:
                                    normalise(turn, m - 1, banks[("o", m - 1)])
                        normalise(turn, STEPS - 1, banks[("o", STEPS - 1)])

                    last_and_turns(dve, body)

                @block.gpsimd
                def _(pool):
                    def split_max(slot, nth, maxed):
                        steps = Steps(pool, split_step, START + nth * 4)
                        pool.wait_ge(max_done, START + maxed)
                        n4, r4 = nm[:, slot], nmr[:, slot]
                        part = [nms[:, slot, :, 4 * t:4 * t + 4] for t in range(3)]
                        apart(pool)
                        steps.done(nc.gpsimd.tensor_copy(part[0], n4))
                        steps.settle()
                        steps.done(nc.gpsimd.tensor_tensor(r4, n4, part[0], ALU.subtract))
                        steps.settle()
                        apart(pool)
                        steps.done(nc.gpsimd.tensor_copy(part[1], r4))
                        steps.settle()
                        steps.done(nc.gpsimd.tensor_tensor(nmr[:, slot], r4, part[1], ALU.subtract))
                        steps.settle()
                        apart(pool)
                        nc.gpsimd.tensor_copy(part[2], r4).then_inc(split, 1)

                    def lay_values(par, batch):
                        apart(pool)
                        nc.gpsimd.tensor_copy(vpad[:, par, :, :, 0:HD].rearrange("p k h d -> p (k h) d"),
                                              v_all[:, batch, :, :].rearrange("p k (h d) -> p (k h) d", d=HD)
                                              ).then_inc(v_ready[par], 1)

                    lay_values(0, 0)
                    for c in range(2):
                        split_max(c, c, (c + 1) * NS)

                    def body(turn, last):
                        k = 0
                        for m in range(STEPS):
                            if m == 0:
                                pool.wait_ge(pv_done, START + turn * 4 * STEPS)
                                lay_values(1, 2 * turn + 1)
                            for kb in range(NB):
                                k += len(exp_uses(causal, kb))
                                if causal:
                                    u = 4 * m + kb
                                    pool.wait_ge(exp_done, START + turn * STEPS * NE + k)
                                    diag = E[:, u % 4, :, 0:128]
                                    apart(pool)
                                    nc.gpsimd.affine_select(out=diag, in_=diag, compare_op=ALU.is_ge, fill=0.0, base=0,
                                                            pattern=[[0, 4], [1, 128]], channel_multiplier=-1
                                                            ).then_inc(tri_done, 1)
                            if m == 4 and not last:
                                pool.wait_ge(pv_done, START + turn * 4 * STEPS + 16)
                                lay_values(0, 2 * turn + 2)
                            if not (last and m + 2 >= STEPS):
                                nth = turn * STEPS + m + 2
                                pool.wait_ge(mT_psum, START + turn * STEPS + m + 1)
                                split_max(m % 2, nth, (nth + 1) * NS)

                    last_and_turns(pool, body)

                @block.sync
                def _(sp):
                    def load(par, batch):
                        for j in range(2):
                            sp.dma_start(qpad[48 * j:48 * j + 48, par, :, 2 * j:2 * j + 2, :].rearrange("r c g s -> r c (g s)"),
                                         q_scr[batch, j].rearrange("t (d c p) s -> (t d) c (p s)", d=HD, c=QUADS)
                                         ).then_inc(qk_load[par], 16)
                        sp.dma_start(kk[0:96, par, :],
                                     k_scr[batch].rearrange("j t (d p) s -> (j t d) (p s)", d=HD)).then_inc(qk_load[par], 16)
                        if not causal:
                            sp.dma_start(qpad[96:98, par].rearrange("r c g s -> r (c g) s"),
                                         m_scr[0:2, batch, :].unsqueeze(1).to_broadcast([2, H, S])).then_inc(qk_load[par], 16)
                            sp.dma_start(kk[96:98, par].rearrange("r (p s) -> r p s", s=S),
                                         m_scr[2:4, batch, :].unsqueeze(1).to_broadcast([2, PAIRS, S])).then_inc(qk_load[par], 16)

                    def store_max(m, nth):
                        par, c = (m // 4) % 2, m % 4
                        sp.wait_ge(mT_ready, START + nth + 1)
                        sp.dma_start(qpad[MAX_ROW:ROWS, par, c], mT[:, m % 2, :]).then_inc(max_row[m % 2], 16)

                    load(0, 0)
                    store_max(0, 0)

                    def body(turn, last):
                        sp.wait_ge(st_ready, START + turn * STEPS * NE)
                        load(1, 2 * turn + 1)
                        for m in range(STEPS):
                            if not (last and m + 1 == STEPS):
                                store_max(m + 1, turn * STEPS + m + 1)
                            if m == 3 and not last:
                                sp.wait_ge(st_ready, START + turn * STEPS * NE + 4 * NE)
                                load(0, 2 * turn + 2)

                    last_and_turns(sp, body)

        CSTEPS = 19

        def class_stage():
            cols = sb("cols", [128, 8])
            big = sb("big", [128, 2, B, NB])
            cls = sb("cls", [128, 3, B, NB])
            rows4 = sb("rows4", [128, 5, B, NB], BF16)
            rowsT = sb("rowsT", [B * NB, 5, 128], BF16)
            ext = sx_all
            penb = E[0:XQ, 2].rearrange("p g s -> p (g s)").bitcast(BF16)
            xm = sb("xm", [XQ, B])
            xsum = sb("xsum", [XQ, B])
            eT = sb("eT", [128, NB, XQ])
            w80 = sb("w80", [XQ, D])
            c_step, red, rT_psum, rT_read = sem("d_step"), sem("d_red"), sem("d_rT_psum"), sem("d_rT_read")
            stored, pen_in, x_step = sem("d_stored"), sem("d_pen_in"), sem("d_x_step")
            xe, xT_, xTr, xo, xw, x5, x5r = (sem("d_x%d" % n) for n in range(7))
            ps_r = work[:, 0, :].bitcast(BF16)

            with nc.Block() as block:
                @block.gpsimd
                def _(pool):
                    nc.gpsimd.memset(cols[:, 0:1], 1.0).then_inc(red, 1)
                    pool.wait_ge(red, 1)
                    apart(pool)
                    nc.gpsimd.affine_select(out=cols[:, 0:1], in_=cols[:, 0:1], compare_op=ALU.is_ge, fill=0.0, base=REG - 1,
                                            pattern=[[0, 1]], channel_multiplier=-1).then_inc(red, 1)
                    pool.wait_ge(c_step, 5)
                    nc.gpsimd.partition_all_reduce(cols[:, 4:6], cols[:, 2:4], 128,
                                                   bass.bass_isa.ReduceOp.max).then_inc(red, 1)

                @block.vector
                def _(dve):
                    s = Steps(dve, c_step)
                    dve.wait_ge(red, 2)
                    s.done(nc.vector.tensor_copy(big[:, 0], sim[:]))
                    s.done(nc.vector.tensor_scalar(big[:, 1], sim[:], -1.0, None, ALU.mult))
                    s.settle()
                    s.done(nc.vector.tensor_scalar(cols[:, 1:2], cols[:, 0:1], -BIG, None, ALU.mult))
                    s.settle()
                    s.done(nc.vector.tensor_scalar(big[:, :, :, 0], big[:, :, :, 0], cols[:, 1:2], None, ALU.add))
                    s.settle()
                    s.done(nc.vector.tensor_reduce(cols[:, 2:4], big[:].rearrange("p a b j -> p a (b j)"), AX.X, ALU.max))
                    dve.wait_ge(red, 3)
                    s.done(nc.vector.tensor_tensor(cols[:, 6:7], cols[:, 4:5], cols[:, 5:6], ALU.add))
                    s.settle()
                    flat = sim[:]
                    s.done(nc.vector.tensor_scalar(cls[:, 0], flat, cols[:, 5:6], None, ALU.add))
                    s.done(nc.vector.reciprocal(cols[:, 6:7], cols[:, 6:7]))
                    s.settle()
                    s.done(nc.vector.tensor_scalar(cls[:, 0], cls[:, 0], cols[:, 6:7], 0.9, ALU.mult, ALU.is_gt))
                    s.settle()
                    s.done(nc.vector.tensor_copy(cls[:, 2], cls[:, 0]))
                    s.settle()
                    s.done(nc.vector.tensor_scalar(cls[:, 0, :, 0], cls[:, 0, :, 0], cols[:, 0:1], None, ALU.max))
                    s.settle()
                    s.done(nc.vector.tensor_scalar(cls[:, 1], cls[:, 0], -1.0, 1.0, ALU.mult, ALU.add))
                    s.done(nc.vector.tensor_scalar(cols[:, 7:8], cols[:, 0:1], -1.0, 1.0, ALU.mult, ALU.add))
                    s.settle()
                    s.done(nc.vector.tensor_scalar(cls[:, 2, :, 0], cls[:, 2, :, 0], cols[:, 7:8], None, ALU.mult))
                    s.settle()
                    s.done(nc.vector.tensor_scalar(rows4[:, 0], cls[:, 1], -BIG, None, ALU.mult))
                    s.done(nc.vector.tensor_scalar(rows4[:, 1], cls[:, 0], -BIG, None, ALU.mult))
                    s.done(nc.vector.tensor_copy(rows4[:, 2], cls[:, 2]))
                    s.done(nc.vector.tensor_copy(rows4[:, 3], cls[:, 1]))
                    s.done(nc.vector.tensor_scalar(rows4[:, 4], cls[:, 2], -BIG, None, ALU.mult))
                    s.settle()
                    assert s.n == CSTEPS, s.n
                    dve.wait_ge(rT_psum, 1)
                    nc.vector.tensor_copy(rowsT[:].rearrange("p k t -> p (k t)"), ps_r[0:B * NB, 0:640]).then_inc(rT_read, 1)

                    dve.wait_ge(pen_in, 16)
                    xs = Steps(dve, x_step)
                    xs.done(nc.vector.tensor_tensor(ext.rearrange("p b s -> p (b s)"), sx_all.rearrange("p b s -> p (b s)"),
                                                    penb, ALU.add))
                    xs.settle()
                    xs.done(nc.vector.tensor_reduce(xm[:], ext, AX.X, ALU.max, negate=True))
                    xs.settle()
                    xs.done(nc.vector.tensor_scalar(xm[:], xm[:], SCALE, None, ALU.mult))
                    for b in range(B):
                        dve.wait_ge(xT_, b + 1)
                        if b:
                            dve.wait_ge(xo, b)
                        nc.vector.tensor_copy(eT[:].rearrange("p k q -> p (k q)"), work[:, 1, 0:NB * XQ]).then_inc(xTr, 1)
                        if b == 0:
                            dve.wait_ge(xe, B)
                            xs.done(nc.vector.reciprocal(xsum[:], xsum[:]))
                            xs.settle()
                        dve.wait_ge(xo, b + 1)
                        if b:
                            dve.wait_ge(x5, b)
                        nc.vector.scalar_tensor_tensor(out=w80[:], in0=work[0:XQ, 2, 0:D], scalar=xsum[:, b:b + 1],
                                                       in1=bd_c[:], op0=ALU.mult, op1=ALU.mult).then_inc(xw, 1)
                        dve.wait_ge(x5, b + 1)
                        nc.vector.tensor_copy(o_neg[:, b, :], pv[0:REG, 0:D]).then_inc(x5r, 1)

                @block.scalar
                def _(act):
                    act.wait_ge(x_step, 3)
                    for b in range(B):
                        nc.scalar.activation(ext[:, b, :], ext[:, b, :], ACT.Exp, scale=SCALE, bias=xm[:, b:b + 1],
                                             accum_out=xsum[:, b:b + 1]).then_inc(xe, 1)

                @block.tensor
                def _(pe):
                    pe.wait_ge(c_step, CSTEPS)
                    for k in range(5):
                        mm = nc.tensor.transpose(ps_r[0:B * NB, k * 128:(k + 1) * 128],
                                                 rows4[:, k].rearrange("p b j -> p (b j)"), id16[:])
                    mm.then_inc(rT_psum, 1)
                    for b in range(B):
                        pe.wait_ge(xe, b + 1)
                        if b:
                            pe.wait_ge(xTr, b)
                        for k in range(NB):
                            mm = nc.tensor.transpose(work[:, 1, k * XQ:(k + 1) * XQ], ext[:, b, k * 128:(k + 1) * 128],
                                                     id32[0:XQ, 0:XQ])
                        mm.then_inc(xT_, 1)
                        pe.wait_ge(xTr, b + 1)
                        if b:
                            pe.wait_ge(xw, b)
                        for k in range(NB):
                            mm = nc.tensor.matmul(work[0:XQ, 2, 0:D], eT[:, k, :], v_all[:, b, k, :],
                                                  start=(k == 0), stop=(k == NB - 1))
                        mm.then_inc(xo, 1)
                        pe.wait_ge(xw, b + 1)
                        if b:
                            pe.wait_ge(x5r, b)
                        nc.tensor.matmul(pv[0:REG, 0:D], selr_sb[:], w80[:], start=True, stop=True).then_inc(x5, 1)

                @block.sync
                def _(sp):
                    sp.wait_ge(rT_read, 1)
                    sp.dma_start(m_scr.rearrange("k b (j t) -> (b j) k t", t=128), rowsT[:]).then_inc(stored, 16)
                    sp.wait_ge(stored, 16)
                    sp.dma_start(penb, m_scr[4:5].rearrange("o b s -> o (b s)").to_broadcast([XQ, B * S])).then_inc(pen_in, 16)
                    sp.wait_ge(pen_in, 16)

        def register_mean():
            r_step = sem("r_step")
            with nc.Block() as block:
                @block.vector
                def _(dve):
                    o = o_all[0:REG, :, 0, :]
                    nc.vector.tensor_tensor(o, o, o_neg[:], ALU.add).then_inc(r_step, 1)
                    dve.wait_ge(r_step, 1)
                    nc.vector.tensor_scalar(o, o, 0.5, None, ALU.mult).then_inc(r_step, 1)

        batch_stage("a_", None, 1)
        attention_stage("b_", True)
        batch_stage("c_", (wo_sb, bo_bc), 2)
        class_stage()
        attention_stage("e_", False)
        register_mean()
        batch_stage("f_", (wp_sb, bp_bc), None)


def kernel(**inputs):
    import ml_dtypes
    import numpy as np
    import concourse.bacc as bacc
    from concourse.bass_utils import run_bass_kernel_spmd as run

    a = {k: np.asarray(v) for k, v in inputs.items()}

    def pair_rows(w):
        return w.reshape((4, 2, 2, HD) + w.shape[1:]).transpose((1, 3, 0, 2) + tuple(range(4, 3 + w.ndim))).reshape(w.shape)

    w2 = a["L0_ffn_W_qkv"]
    head = pair_rows(np.repeat(np.arange(H), HD))
    cols = np.repeat(np.arange(H), REG)
    arrays = {
        "x": a["L0_attn_x"],
        "wqT": pair_rows(a["L0_attn_Wq"]).T, "wkT": pair_rows(a["L0_attn_Wk"]).T,
        "wvT": a["L0_attn_Wv"].T, "woT": a["L0_attn_Wo"].T,
        "bq": pair_rows(a["L0_attn_bq"])[:, None], "bk": pair_rows(a["L0_attn_bk"])[:, None],
        "bv": a["L0_attn_bv"][None, :], "bo": a["L0_attn_bo"][None, :],
        "g_info": a["L0_ffn_g_info"][0, 0:1, :],
        "w2q": np.concatenate([w2[:, 0:D], pair_rows(w2[:, 0:D].T).T], axis=1),
        "w2k": pair_rows(w2[:, D:2 * D].T).T, "w2v": w2[:, 2 * D:3 * D],
        "wpT": a["L0_ffn_W_proj"], "bp": a["L0_ffn_b_proj"][None, :],
        "ident": np.eye(128, dtype=np.float32),
        "tri": np.triu(np.full((128, 128), -BIG, dtype=np.float32), 1).astype(ml_dtypes.bfloat16),
        "bd_rows": (head[:, None] == cols[None, :]).astype(np.float32),
        "bd_cols": (cols[:, None] == np.repeat(np.arange(H), HD)[None, :]).astype(np.float32),
        "sel_r": (np.tile(np.arange(REG), H)[:, None] == np.arange(REG)[None, :]).astype(np.float32),
    }
    arrays = {k: np.ascontiguousarray(v) for k, v in arrays.items()}
    nc = bacc.Bacc("TRN2", target_bir_lowering=False, num_devices=1)
    aps = {k: nc.dram_tensor(k, v.shape, mybir.dt.from_np(v.dtype), kind="ExternalInput").ap() for k, v in arrays.items()}
    out = nc.dram_tensor("out", (B, S, D), F32, kind="ExternalOutput").ap()
    build(nc, out=out, **aps)
    r = run(nc, [arrays], core_ids=[0])
    return r.results[0]["out"]
```

```python
from contextlib import ExitStack

import concourse.bass as bass
from concourse import mybir

F32 = mybir.dt.float32
BF16 = mybir.dt.bfloat16
U32 = mybir.dt.uint32
I32 = mybir.dt.int32
ALU = mybir.AluOpType
ACT = mybir.ActivationFunctionType
AX = mybir.AxisListType

B, S, D, H, HD = 8, 512, 128, 16, 8
REG = 5
NB = S // 128
PAIRS, QUADS = H // 2, H // 4
TERMS = 6
MASK_ROW = 2 * TERMS * HD
MAX_ROW = MASK_ROW + 2
ROWS = MAX_ROW + 3
VW = 32
SCALE = 1.0 / float(HD) ** 0.5
BIG = 1.0e30
EPS = 1e-5
RSQRT_BITS = float(0x5f3759df)
XQ = H * REG
STEPS = 2 * QUADS
TURNS = B // 2
START = 16
Q_TERMS = (0, 1, 0, 1, 1, 2)
K_TERMS = (0, 1, 1, 0, 2, 1)


class Steps:

    def __init__(self, eng, sem, base=0):
        self.eng, self.sem, self.base, self.n = eng, sem, base, 0

    def done(self, ins):
        ins.then_inc(self.sem, 1)
        self.n += 1

    def settle(self):
        self.eng.wait_ge(self.sem, self.base + self.n)


def score_uses(causal):
    if not causal:
        return [(i, [g], S) for i in range(NB) for g in range(4)]
    return ([(3, [g], 512) for g in range(4)] + [(2, [g], 384) for g in range(4)]
            + [(1, [0, 1], 256), (1, [2, 3], 256), (0, [0, 1, 2, 3], 128)])


def exp_uses(causal, kb):
    if not causal or kb == 0:
        return [([0, 1], 512, 512), ([2, 3], 512, 512)]
    if kb == 1:
        return [([0, 1], 384, 512), ([2, 3], 384, 512)]
    if kb == 2:
        return [([0, 1, 2, 3], 256, 256)]
    return [([0, 1, 2, 3], 128, 128)]


PREP1_EVEN = [("xn_stats", 0, 0), ("xn", 0, 1), ("xT", 0, 2), ("qk", 0, 3), ("tok", 1, 0)] \
    + [("split%d" % n, 1 + n // 4, n % 4) for n in range(6)]
PREP1_ODD = [("xn_stats", 2, 2), ("xn", 2, 3), ("xT", 3, 0), ("qk", 4, 1), ("tok", 4, 1)] \
    + [("split%d" % n, 4 + (n + 2) // 4, (n + 2) % 4) for n in range(6)]
POST_ODD = [("reg", 0, 3), ("oT", 1, 0), ("y", 1, 1), ("x_new", 1, 2)]
PREP2_ODD = [("xn_stats", 1, 3), ("xn", 2, 0), ("xT", 2, 1), ("qk", 2, 2), ("tok", 2, 3), ("qbd", 2, 3), ("sx", 3, 0)] \
    + [("split%d" % n, 2 + (n + 3) // 4, (n + 3) % 4) for n in range(6)] + [("sim0", 3, 1), ("sim1", 3, 2), ("sim2", 3, 3)]
POST_EVEN = [("reg", 4, 2), ("oT", 4, 3), ("y", 5, 0), ("x_new", 5, 1)]
PREP2_EVEN = [("xn_stats", 5, 2), ("xn", 5, 3), ("xT", 6, 0), ("qk", 6, 1), ("tok", 6, 2), ("qbd", 6, 2), ("sx", 6, 3)] \
    + [("split%d" % n, 6 + (n + 2) // 4, (n + 2) % 4) for n in range(6)] + [("sim0", 7, 0), ("sim1", 7, 1), ("sim2", 7, 2)]

SIGNALS = ("st_ready exp_done tri_done s_ready max_done split split_step mT_psum mT_ready max_row0 max_row1 "
           "pv_done pv_read oT_psum rec_done o_done qk_load0 qk_load1 v_ready0 v_ready1 "
           "dve_step pow_done xn_ready xT_psum xT_ready qk_psum qk_read tok_psum tok_read tokq_read part_done stored "
           "qbd_ready sx_psum sx_read sim_pool sim_dve post_psum post_read y_psum y_read x_done reg_step out_done").split()
BANK_READ = {"S": "max_done", "mT": "mT_ready", "OT": "o_done", "xT": "xT_ready", "qk": "qk_read", "tok": "tok_read",
             "sx": "sx_read", "oT": "post_read", "y": "y_read"}


MAXIMA_AT = {False: [range(4 * kb, 4 * kb + 4) for kb in range(NB)],
             True: [range(0, 2), range(2, 5), range(5, 8), range(8, 11)]}


class Step:

    def __init__(self, kind, m=0, kb=0, batch=0, two=False, use=0):
        self.kind, self.m, self.kb, self.batch, self.two, self.use = kind, m, kb, batch, two, use


def work_of(pieces, batch, two, m=None, kb=None):
    return [Step(k, batch=batch, two=two) for k, pm, pk in pieces if m is None or (pm, pk) == (m, kb)]


def turn_steps(causal, first, last):
    steps = [Step("load", batch=1), Step("lay", batch=1)]
    for m in range(STEPS):
        for kb in range(NB):
            if (m, kb) == (4, 0) and not last:
                steps.append(Step("load", batch=2))
            others = [Step("ST", m, kb, use=n) for n in range(len(exp_uses(causal, kb)))]
            if 4 * m + kb > 0:
                others.append(Step("PV", (4 * m + kb - 1) // 4, (kb - 1) % 4))
            maxima = [] if last and m + 2 >= STEPS else [Step("S", m + 2, use=n) for n in MAXIMA_AT[causal][kb]]
            for n in range(max(len(maxima), len(others))):
                steps += maxima[n:n + 1] + others[n:n + 1]
            if (m, kb) == (4, 0) and not last:
                steps.append(Step("lay", batch=2))
            if kb == 1 and not (last and m + 1 == STEPS):
                steps.append(Step("mT", m + 1))
            if kb == 2 and m > 0:
                steps.append(Step("OT", m - 1))
            if causal and not last:
                steps += work_of(PREP1_EVEN, 2, False, m, kb) + work_of(PREP1_ODD, 3, False, m, kb)
            if not first:
                steps += work_of(POST_ODD, -1, True, m, kb) + (work_of(PREP2_ODD, -1, True, m, kb) if causal else [])
            steps += work_of(POST_EVEN, 0, True, m, kb) + (work_of(PREP2_EVEN, 0, True, m, kb) if causal else [])
    return steps + [Step("PV", STEPS - 1, NB - 1), Step("OT", STEPS - 1)]


def ahead_steps(causal):
    steps = work_of(PREP1_EVEN, 0, False) if causal else []
    steps += [Step("load", batch=0), Step("lay", batch=0)]
    steps += work_of(PREP1_ODD, 1, False) if causal else []
    steps += [Step("S", c, use=n) for c in range(2) for n in range(len(score_uses(causal)))]
    return steps + [Step("mT", 0)]


def after_steps(causal):
    return work_of(POST_ODD, 1, True) + (work_of(PREP2_ODD, 1, True) if causal else [])


def counts(step, causal):
    k, two = step.kind, step.two
    if k == "ST":
        return {"st_ready": 1, "exp_done": 1, "tri_done": int(causal and step.use == len(exp_uses(causal, step.kb)) - 1)}
    if k == "S":
        over = int(step.use == len(score_uses(causal)) - 1)
        return {"s_ready": 1, "max_done": 1, "split": over, "split_step": 4 * over}
    if k == "PV":
        return {"pv_done": 1, "pv_read": int(step.kb == 3)}
    if k == "mT":
        return {"mT_psum": 1, "mT_ready": 1, "max_row%d" % (step.m % 2): 16}
    if k.startswith("split"):
        return {"part_done": 1, "stored": 16 * TERMS if k in ("split2", "split5") else 0}
    return {
        "OT": {"oT_psum": 1, "rec_done": 1, "o_done": 1},
        "load": {"qk_load%d" % (step.batch % 2): 16 * (3 if causal else 5)},
        "lay": {"v_ready%d" % (step.batch % 2): 1},
        "xn_stats": {"dve_step": 2 * NB + 1, "pow_done": 1},
        "xn": {"xn_ready": NB},
        "xT": {"xT_psum": 1, "xT_ready": 1},
        "qk": {"qk_psum": 2, "qk_read": 4},
        "tok": {"tok_psum": 1 + two, "tok_read": 1 + two},
        "qbd": {"qbd_ready": 1},
        "sx": {"sx_psum": 1, "sx_read": 1},
        "sim0": {"sim_pool": 2},
        "sim1": {"sim_dve": 2},
        "sim2": {"sim_dve": 12},
        "reg": {} if causal else {"reg_step": 2},
        "oT": {"post_psum": 1, "post_read": 1},
        "y": {"y_psum": 1, "y_read": 1, "dve_step": 2 * NB + 1, "pow_done": 1},
        "x_new": {"dve_step": NB, "x_done": 1, "out_done": 0 if causal else 16},
    }[k]


def banks_of(step, causal):
    k = step.kind
    return (2 if k == "qk" else 1 + step.two if k == "tok"
            else 1 if k in BANK_READ else 0)


class Part:

    def __init__(self, steps, causal, before):
        self.steps, self.start, self.causal = steps, before, causal
        self.before, self.banks, self.by = [], [], {}
        local, ring = dict.fromkeys(SIGNALS, 0), 0
        for n, step in enumerate(steps):
            self.before.append(dict(local))
            for name, k in counts(step, causal).items():
                local[name] += k
            used = banks_of(step, causal)
            self.banks.append([(ring + b) % 3 for b in range(used)])
            ring += used
            step.n = n
            self.by[step.kind, step.m, step.kb] = step
        self.total = local
        self.each_turn, self.turn, self.first_turn = dict.fromkeys(SIGNALS, 0), 0, 0

    def after(self):
        return {k: self.start[k] + self.total[k] for k in SIGNALS}

    def at(self, turn, looped=0):
        self.turn, self.looped = turn, looped
        return self

    def upto(self, name, step):
        v = START + self.start[name] + self.before[step.n][name]
        if self.looped and self.total[name]:
            v = (self.turn - self.looped) * self.total[name] + v
        return v

    def through(self, name, step):
        return self.upto(name, step) + counts(step, self.causal).get(name, 0)


def build(nc, x, wqT, wkT, wvT, woT, bq, bk, bv, bo, g_info, w2q, w2k, w2v, wpT, bp, ident, tri, bd_rows, bd_cols, sel_r,
          out):
    with ExitStack() as ctx:
        def sb(name, shape, dt=F32):
            return ctx.enter_context(nc.sbuf_tensor(name, shape, dt))

        def sem(name):
            return ctx.enter_context(nc.semaphore(name))

        def dram(name, shape, dt):
            return nc.dram_tensor(name, shape, dt).ap()

        x_all = sb("x_all", [128, B, NB, D])
        v_all = sb("v_all", [128, B, NB, D])
        o_turn = sb("o_turn", [128, 2, NB, D])
        qpad = sb("qpad", [128, 2, QUADS, 4, S], BF16)
        kk = sb("kk", [128, 2, PAIRS * S], BF16)
        vpad = sb("vpad", [128, 2, NB, H, VW])
        E = sb("E", [128, 4, 4, S])
        id32 = sb("id32", [128, 128])
        id16 = sb("id16", [128, 128], BF16)
        tri_sb = sb("tri_sb", [128, 128], BF16)
        wq_sb = sb("wq_sb", [128, D])
        wk_sb = sb("wk_sb", [128, D])
        wqv_sb = sb("wqv_sb", [128, 2 * D])
        wo_sb = sb("wo_sb", [128, D])
        bq_sb = sb("bq_sb", [128, 1])
        bk_sb = sb("bk_sb", [128, 1])
        bv_bc = sb("bv_bc", [128, D])
        bo_bc = sb("bo_bc", [128, D])
        w2q_sb = sb("w2q_sb", [128, D])
        w2k_sb = sb("w2k_sb", [128, D])
        w2v_sb = sb("w2v_sb", [128, 2 * D])
        wp_sb = sb("wp_sb", [128, D])
        bp_bc = sb("bp_bc", [128, D])
        g_bc = sb("g_bc", [128, D])
        g_n = sb("g_n", [128, H])
        mhalf = sb("mhalf", [128, H])
        bd_r = sb("bd_r", [128, H, REG])
        bd_c = sb("bd_c", [XQ, D])
        selr_sb = sb("selr_sb", [XQ, REG])
        sim = sb("sim", [128, B, NB])
        sx_all = sb("sx_all", [XQ, B, S])
        o_neg = sb("o_neg", [REG, B, D])
        xn = sb("xn", [128, NB, D])
        xT = sb("xT", [128, S])
        qf = sb("qf", [128, S])
        kf = sb("kf", [128, S])
        res = sb("res", [128, S])
        parts = sb("parts", [128, 2, 3, S], BF16)
        stats = sb("stats", [128, NB, 6])
        mv = sb("mv", [128, NB, 2])
        rstd = sb("rstd", [128, NB])
        y_sb = sb("y_sb", [128, NB, D])
        oT2 = sb("oT2", [128, S])
        qtok = sb("qtok", [128, NB * D])
        prod = sb("prod", [128, 2, NB * D])
        dots = sb("dots", [128, NB * H])
        nrm2 = sb("nrm2", [128, NB * H])
        rs = sb("rs", [128, NB * H])
        rs2 = sb("rs2", [128, NB * H])
        qbd = sb("qbd", [128, H, REG])
        nm = sb("nm", [128, 2, NB, 4])
        nmr = sb("nmr", [128, 2, NB, 4])
        nms = sb("nms", [128, 2, NB, 12], BF16)
        mT = sb("mT", [12, 2, S], BF16)
        oT = sb("oT", [128, 2, S])
        rec = sb("rec", [128, NB, 4])

        work = ctx.enter_context(nc.psum_tensor("work", [128, 3, 512], F32))
        st = ctx.enter_context(nc.psum_tensor("st", [128, 2, 1024], F32))
        pv = ctx.enter_context(nc.psum_tensor("pv", [128, 512], F32))

        q_scr = {c: dram("q_scr%d" % c, [B, 2, TERMS, 64, S], BF16) for c in (True, False)}
        k_scr = {c: dram("k_scr%d" % c, [B, 2, TERMS, 64, S], BF16) for c in (True, False)}
        m_scr = dram("m_scr", [5, B, S], BF16)

        signal = {tag + name: sem(tag + name) for tag in ("p1_", "p2_") for name in SIGNALS}

        loaded = sem("loaded")
        held = sem("held")
        cleared, halves, v_zero, k_ones = sem("cleared"), sem("halves"), sem("v_zero"), sem("k_ones")
        g_step, g_pow = sem("g_step"), sem("g_pow")
        with nc.Block() as block:
            @block.sync
            def _(sp):
                loads = [(wq_sb[:], wqT), (wk_sb[:], wkT), (wqv_sb[:, 0:D], wvT), (wo_sb[:], woT),
                         (bq_sb[:], bq), (bk_sb[:], bk),
                         (bv_bc[:], bv.to_broadcast([128, D])), (bo_bc[:], bo.to_broadcast([128, D])),
                         (w2q_sb[:], w2q[:, D:2 * D]), (w2k_sb[:], w2k), (w2v_sb[:, 0:D], w2v), (w2v_sb[:, D:2 * D], w2q[:, 0:D]),
                         (wp_sb[:], wpT), (bp_bc[:], bp.to_broadcast([128, D])),
                         (g_bc[:], g_info.to_broadcast([128, D])),
                         (id32[:], ident), (tri_sb[:], tri), (bd_r[:].rearrange("p h r -> p (h r)"), bd_rows),
                         (bd_c[:], bd_cols), (selr_sb[:], sel_r)]
                loads += [(x_all[:, b, :, :], x[b].rearrange("(j p) d -> p j d", p=128)) for b in range(B)]
                for dst, src in loads:
                    sp.dma_start(dst, src).then_inc(loaded, 16)
                for s in signal.values():
                    sp.sem_inc(s, START)
                sp.wait_ge(loaded, 16 * len(loads))

            @block.vector
            def _(dve):
                nc.vector.memset(qpad[:].bitcast(U32), 0).then_inc(cleared, 1)
                steps = Steps(dve, g_step)
                n_loads = 20 + B
                dve.wait_ge(loaded, 16 * n_loads)
                nc.vector.tensor_copy(id16[:], id32[:]).then_inc(cleared, 1)
                steps.done(nc.vector.tensor_tensor(prod[:, 0, 0:D], g_bc[:], g_bc[:], ALU.mult))
                steps.settle()
                steps.done(nc.vector.tensor_reduce(g_n[:], prod[:, 0, 0:D].rearrange("p (h d) -> p h d", d=HD),
                                                   AX.X, ALU.add))
                steps.settle()
                dve.wait_ge(g_pow, 1)
                g3 = g_bc[:].rearrange("p (h d) -> p h d", d=HD)
                steps.done(nc.vector.tensor_tensor(g3, g3, g_n[:].unsqueeze(2).to_broadcast([128, H, HD]), ALU.mult))

            @block.gpsimd
            def _(pool):
                nc.gpsimd.memset(kk[MASK_ROW:ROWS], 1.0).then_inc(k_ones, 1)
                pool.wait_ge(k_ones, 1)
                nc.gpsimd.memset(mhalf[:], -0.5).then_inc(halves, 1)
                nc.gpsimd.memset(vpad[:], 0.0).then_inc(v_zero, 1)
                pool.wait_ge(v_zero, 1)
                nc.gpsimd.memset(vpad[:, :, :, :, HD:HD + 1].rearrange("p a k h o -> p (a k h) o"), 1.0).then_inc(cleared, 1)
                pool.wait_ge(halves, 1)
                pool.wait_ge(g_step, 2)
                nc.gpsimd.tensor_tensor(g_n[:], g_n[:], mhalf[:, 0:H], ALU.pow).then_inc(g_pow, 1)

        def apart(eng):
            eng.sem_inc(held, 1)

        def phase(tag, causal):
            g = {name: signal[tag + name] for name in SIGNALS}
            n_uses = len(score_uses(causal))
            post_w, post_b = (wo_sb, bo_bc) if causal else (wp_sb, bp_bc)

            zero = dict.fromkeys(SIGNALS, 0)
            ahead = Part(ahead_steps(causal), causal, zero)
            first = Part(turn_steps(causal, True, False), causal, ahead.after())
            middle = Part(turn_steps(causal, False, False), causal, first.after())
            middle_end = {k: middle.start[k] + (TURNS - 2) * middle.total[k] for k in SIGNALS}
            last = Part(turn_steps(causal, False, True), causal, middle_end)
            after = Part(after_steps(causal), causal, last.after())

            def go(eng, part_work):
                part_work(ahead.at(0))
                part_work(first.at(0))
                with eng.Fori(1, TURNS - 1) as turn:
                    part_work(middle.at(turn, 1))
                part_work(last.at(TURNS - 1))
                part_work(after.at(TURNS - 1))

            def st_pair(part, step):
                return st[:, part.before[step.n]["exp_done"] % 2, :]

            with nc.Block() as block:
                @block.tensor
                def _(pe):
                    def part_work(part):
                        up, thru = part.upto, part.through
                        for name in sorted(set(BANK_READ.values())):
                            if part.steps and (causal or name in ("max_done", "mT_ready", "o_done", "post_read", "y_read")):
                                pe.wait_ge(g[name], up(name, part.steps[0]))
                        holder = [None] * 3

                        def take(step, k, value):
                            w = part.banks[step.n][k]
                            if holder[w]:
                                pe.wait_ge(*holder[w])
                            holder[w] = (g[BANK_READ[step.kind]], value)
                            return work[:, w, :]

                        for step in part.steps:
                            kind, m, kb = step.kind, step.m, step.kb
                            par, c = (m // 4) % 2, m % 4
                            wq_, wk_, wv_ = (w2q_sb, w2k_sb, w2v_sb) if step.two else (wq_sb, wk_sb, wqv_sb)
                            if kind == "S":
                                if step.use == 0 and c == 0:
                                    name = "qk_load%d" % par
                                    pe.wait_ge(g[name], up(name, step))
                                i, heads, keys = score_uses(causal)[step.use]
                                bank = take(step, 0, thru("max_done", step))
                                for k, h in enumerate(heads):
                                    p = 2 * c + h % 2
                                    o = bank[:, k * keys:(k + 1) * keys]
                                    mm = nc.tensor.matmul(o, qpad[0:MAX_ROW, par, c, h, i * 128:(i + 1) * 128],
                                                          kk[0:MAX_ROW, par, p * S:p * S + keys], start=True,
                                                          stop=not causal)
                                    if causal:
                                        mm = nc.tensor.matmul(o[:, keys - 128:keys], id16[:], tri_sb[:],
                                                              start=False, stop=True)
                                mm.then_inc(g["s_ready"], 1)
                            elif kind == "mT":
                                bank = take(step, 0, thru("mT_ready", step)).bitcast(BF16)
                                pe.wait_ge(g["split"], up("split", step))
                                for i in range(NB):
                                    mm = nc.tensor.transpose(bank[0:12, i * 128:(i + 1) * 128], nms[:, m % 2, i, :], id16[:])
                                mm.then_inc(g["mT_psum"], 1)
                            elif kind == "ST":
                                if kb == 0 and step.use == 0:
                                    name = "max_row%d" % (m % 2)
                                    pe.wait_ge(g[name], up(name, step))
                                heads, queries, stride = exp_uses(causal, kb)[step.use]
                                pe.wait_ge(g["exp_done"], up("exp_done", step) - 1)
                                pair = st_pair(part, step)
                                for a, h in enumerate(heads):
                                    p = 2 * c + h % 2
                                    mm = nc.tensor.matmul(pair[:, a * stride:a * stride + queries],
                                                          kk[0:ROWS, par, p * S + kb * 128:p * S + (kb + 1) * 128],
                                                          qpad[0:ROWS, par, c, h, S - queries:S], start=True, stop=True)
                                mm.then_inc(g["st_ready"], 1)
                            elif kind == "PV":
                                made = part.by["ST", m, kb]
                                if kb == 0:
                                    pe.wait_ge(g["pv_read"], up("pv_read", step))
                                    if c == 0:
                                        name = "v_ready%d" % par
                                        pe.wait_ge(g[name], up(name, step))
                                if causal:
                                    pe.wait_ge(g["tri_done"], thru("tri_done", made))
                                pe.wait_ge(g["exp_done"], thru("exp_done", made))
                                lo = kb * 128 if causal else 0
                                for h in range(4):
                                    mm = nc.tensor.matmul(pv[32 * h:32 * h + VW, lo:S], vpad[:, par, kb, 4 * c + h, :],
                                                          E[:, kb, h, 0:S - lo], start=(kb == 0), stop=(kb == NB - 1),
                                                          tile_position=(0, 32 * h), skip_group_check=True)
                                mm.then_inc(g["pv_done"], 1)
                            elif kind == "OT":
                                bank = take(step, 0, thru("o_done", step))
                                pe.wait_ge(g["pv_read"], up("pv_read", step))
                                for i in range(NB):
                                    mm = nc.tensor.transpose(bank[:, i * 128:(i + 1) * 128],
                                                             oT[:, m % 2, i * 128:(i + 1) * 128], id32[:])
                                mm.then_inc(g["oT_psum"], 1)
                            elif kind == "oT":
                                bank = take(step, 0, thru("post_read", step))
                                pe.wait_ge(g["o_done"], up("o_done", step))
                                if not causal:
                                    pe.wait_ge(g["reg_step"], up("reg_step", step))
                                for j in range(NB):
                                    mm = nc.tensor.transpose(bank[:, j * 128:(j + 1) * 128], o_turn[:, step.batch % 2, j, :],
                                                             id32[:])
                                mm.then_inc(g["post_psum"], 1)
                            elif kind == "y":
                                bank = take(step, 0, thru("y_read", step))
                                pe.wait_ge(g["post_read"], up("post_read", step))
                                for j in range(NB):
                                    mm = nc.tensor.matmul(bank[:, j * 128:(j + 1) * 128], oT2[:, j * 128:(j + 1) * 128],
                                                          post_w[:], start=True, stop=True)
                                mm.then_inc(g["y_psum"], 1)
                            elif kind == "xT":
                                bank = take(step, 0, thru("xT_ready", step))
                                pe.wait_ge(g["xn_ready"], up("xn_ready", step))
                                for j in range(NB):
                                    mm = nc.tensor.transpose(bank[:, j * 128:(j + 1) * 128], xn[:, j, :], id32[:])
                                mm.then_inc(g["xT_psum"], 1)
                            elif kind == "qk":
                                pe.wait_ge(g["xT_ready"], up("xT_ready", step))
                                for k, w in enumerate((wq_, wk_)):
                                    bank = take(step, k, up("qk_read", step) + 2 * k + 2)
                                    nc.tensor.matmul(bank, w[:], xT[:], start=True, stop=True).then_inc(g["qk_psum"], 1)
                            elif kind == "tok":
                                for k in range(1 + step.two):
                                    bank = take(step, k, up("tok_read", step) + k + 1)
                                    for j in range(NB):
                                        mm = nc.tensor.matmul(bank[:, j * 128:(j + 1) * 128], xT[:, j * 128:(j + 1) * 128],
                                                              wv_[:, k * D:(k + 1) * D], start=True, stop=True)
                                    mm.then_inc(g["tok_psum"], 1)
                            elif kind == "sx":
                                bank = take(step, 0, thru("sx_read", step))
                                pe.wait_ge(g["qbd_ready"], up("qbd_ready", step))
                                pe.wait_ge(g["qk_read"], up("qk_read", step))
                                nc.tensor.matmul(bank[0:XQ, :], qbd[:].rearrange("p h r -> p (h r)"), kf[:],
                                                 start=True, stop=True).then_inc(g["sx_psum"], 1)

                    go(pe, part_work)

                @block.scalar
                def _(act):
                    def part_work(part):
                        up, thru = part.upto, part.through
                        for step in part.steps:
                            kind, m, kb = step.kind, step.m, step.kb
                            banks = part.banks[step.n]
                            batch = 2 * part.turn + step.batch
                            if kind == "ST":
                                heads, queries, stride = exp_uses(causal, kb)[step.use]
                                if step.use == 0:
                                    act.wait_ge(g["pv_done"], up("pv_done", step) - 2)
                                act.wait_ge(g["st_ready"], thru("st_ready", step))
                                src = st_pair(part, step)[:, 0:stride * len(heads)].rearrange("p (h q) -> p h q", q=stride)
                                nc.scalar.activation(E[:, kb, heads[0]:heads[-1] + 1, 0:queries],
                                                     src[:, :, 0:queries], ACT.Exp, scale=SCALE
                                                     ).then_inc(g["exp_done"], 1)
                            elif kind == "PV" and kb == 3:
                                act.wait_ge(g["pv_done"], thru("pv_done", step))
                                act.wait_ge(g["oT_psum"], up("oT_psum", step))
                                nc.scalar.copy(oT[:, m % 2, :], pv[:]).then_inc(g["pv_read"], 1)
                            elif kind == "mT":
                                act.wait_ge(g["mT_psum"], thru("mT_psum", step))
                                name = "max_row%d" % (m % 2)
                                act.wait_ge(g[name], up(name, step))
                                nc.scalar.copy(mT[:, m % 2, :], work[:, banks[0], :].bitcast(BF16)[0:12, 0:512]
                                               ).then_inc(g["mT_ready"], 1)
                            elif kind == "oT":
                                act.wait_ge(g["post_psum"], thru("post_psum", step))
                                act.wait_ge(g["y_psum"], up("y_psum", step))
                                nc.scalar.copy(oT2[:], work[:, banks[0], :]).then_inc(g["post_read"], 1)
                            elif kind == "xT":
                                act.wait_ge(g["xT_psum"], thru("xT_psum", step))
                                act.wait_ge(g["tok_psum"], up("tok_psum", step))
                                nc.scalar.copy(xT[:], work[:, banks[0], :]).then_inc(g["xT_ready"], 1)
                            elif kind == "qk":
                                act.wait_ge(g["part_done"], up("part_done", step))
                                act.wait_ge(g["stored"], up("stored", step))
                                act.wait_ge(g["qbd_ready"], up("qbd_ready", step))
                                act.wait_ge(g["sx_psum"], up("sx_psum", step))
                                for k, (dst, bias) in enumerate(((qf, bq_sb), (kf, bk_sb))):
                                    act.wait_ge(g["qk_psum"], up("qk_psum", step) + k + 1)
                                    for o in (dst[:], parts[:, k, 1, :]):
                                        if step.two:
                                            ins = nc.scalar.copy(o, work[:, banks[k], :])
                                        else:
                                            ins = nc.scalar.activation(o, work[:, banks[k], :], ACT.Identity, bias=bias[:])
                                        ins.then_inc(g["qk_read"], 1)
                            elif kind == "tok" and step.two:
                                act.wait_ge(g["tok_psum"], up("tok_psum", step) + 1)
                                w3 = work[:, banks[0], :].rearrange("p (j d) -> p j d", d=D)
                                nc.scalar.copy(v_all[:, batch, :, :], w3).then_inc(g["tok_read"], 1)
                                act.wait_ge(g["tok_psum"], up("tok_psum", step) + 2)
                                act.wait_ge(g["sim_pool"], up("sim_pool", step))
                                nc.scalar.copy(qtok[:], work[:, banks[1], :]).then_inc(g["tok_read"], 1)
                            elif kind == "sx":
                                act.wait_ge(g["sx_psum"], thru("sx_psum", step))
                                nc.scalar.copy(sx_all[:, batch, :], work[0:XQ, banks[0], :]).then_inc(g["sx_read"], 1)

                    go(act, part_work)

                @block.vector
                def _(dve):
                    def statistics(steps, src):
                        for j in range(NB):
                            steps.done(nc.vector.bn_stats(stats[:, j, :], src[:, j, :]))
                        steps.settle()
                        apart(dve)
                        for j in range(NB):
                            steps.done(nc.vector.bn_aggr(mv[:, j, :], stats[:, j, :]))
                        steps.settle()
                        steps.done(nc.vector.tensor_scalar(rstd[:], mv[:, :, 1], EPS, None, ALU.add))

                    def part_work(part):
                        up, thru = part.upto, part.through
                        for step in part.steps:
                            kind, m, kb = step.kind, step.m, step.kb
                            banks = part.banks[step.n]
                            batch = 2 * part.turn + step.batch
                            par, c = (m // 4) % 2, m % 4
                            if kind == "S":
                                if step.use == 0:
                                    dve.wait_ge(g["split"], up("split", step) - 1)
                                i, heads, keys = score_uses(causal)[step.use]
                                dve.wait_ge(g["s_ready"], thru("s_ready", step))
                                src = work[:, banks[0], 0:keys * len(heads)].rearrange("p (h k) -> p h k", k=keys)
                                nc.vector.tensor_reduce(nm[:, m % 2, i, heads[0]:heads[-1] + 1], src, AX.X, ALU.max,
                                                        negate=True).then_inc(g["max_done"], 1)
                            elif kind == "OT":
                                o4 = work[:, banks[0], :].rearrange("p (i g r) -> p i g r", i=NB, g=4)
                                dve.wait_ge(g["oT_psum"], thru("oT_psum", step))
                                dve.wait_ge(g["o_done"], up("o_done", step))
                                nc.vector.reciprocal(rec[:], o4[:, :, :, HD]).then_inc(g["rec_done"], 1)
                                dve.wait_ge(g["rec_done"], thru("rec_done", step))
                                dve.wait_ge(g["post_psum"], up("post_psum", step))
                                dst = o_turn[:, par, :, 4 * HD * c:4 * HD * (c + 1)].rearrange("p i (g d) -> p i g d", d=HD)
                                nc.vector.tensor_tensor(dst, o4[:, :, :, 0:HD],
                                                        rec[:].unsqueeze(3).to_broadcast([128, NB, 4, HD]),
                                                        ALU.mult).then_inc(g["o_done"], 1)
                            elif kind == "reg" and not causal:
                                o = o_turn[0:REG, step.batch % 2, 0, :]
                                dve.wait_ge(g["o_done"], up("o_done", step))
                                nc.vector.tensor_tensor(o, o, o_neg[:, batch, :], ALU.add).then_inc(g["reg_step"], 1)
                                dve.wait_ge(g["reg_step"], up("reg_step", step) + 1)
                                nc.vector.tensor_scalar(o, o, 0.5, None, ALU.mult).then_inc(g["reg_step"], 1)
                            elif kind == "y":
                                steps = Steps(dve, g["dve_step"], up("dve_step", step))
                                steps.settle()
                                dve.wait_ge(g["xn_ready"], up("xn_ready", step))
                                dve.wait_ge(g["x_done"], up("x_done", step))
                                dve.wait_ge(g["y_psum"], thru("y_psum", step))
                                nc.vector.tensor_tensor(y_sb[:], work[:, banks[0], :].rearrange("p (j d) -> p j d", d=D),
                                                        post_b[:].unsqueeze(1).to_broadcast([128, NB, D]),
                                                        ALU.add).then_inc(g["y_read"], 1)
                                dve.wait_ge(g["y_read"], thru("y_read", step))
                                apart(dve)
                                statistics(steps, y_sb)
                            elif kind == "x_new":
                                steps = Steps(dve, g["dve_step"], up("dve_step", step))
                                dve.wait_ge(g["pow_done"], up("pow_done", step))
                                for j in range(NB):
                                    steps.done(nc.vector.tensor_scalar(y_sb[:, j, :], y_sb[:, j, :], mv[:, j, 0:1],
                                                                       rstd[:, j:j + 1], ALU.subtract, ALU.mult))
                                steps.settle()
                                nc.vector.tensor_tensor(x_all[:, batch, :, :], x_all[:, batch, :, :], y_sb[:],
                                                        ALU.add).then_inc(g["x_done"], 1)
                            elif kind == "xn_stats":
                                steps = Steps(dve, g["dve_step"], up("dve_step", step))
                                steps.settle()
                                dve.wait_ge(g["x_done"], up("x_done", step))
                                dve.wait_ge(g["xn_ready"], up("xn_ready", step))
                                apart(dve)
                                statistics(steps, x_all[:, batch, :, :])
                            elif kind == "xn":
                                dve.wait_ge(g["xT_psum"], up("xT_psum", step))
                                dve.wait_ge(g["pow_done"], up("pow_done", step))
                                for j in range(NB):
                                    nc.vector.tensor_scalar(xn[:, j, :], x_all[:, batch, j, :], mv[:, j, 0:1], rstd[:, j:j + 1],
                                                            ALU.subtract, ALU.mult).then_inc(g["xn_ready"], 1)
                            elif kind == "tok" and not step.two:
                                dve.wait_ge(g["tok_psum"], thru("tok_psum", step))
                                w3 = work[:, banks[0], :].rearrange("p (j d) -> p j d", d=D)
                                nc.vector.tensor_tensor(v_all[:, batch, :, :], w3, bv_bc[:].unsqueeze(1).to_broadcast([128, NB, D]),
                                                        ALU.add).then_inc(g["tok_read"], 1)
                            elif kind == "qbd":
                                dve.wait_ge(g["qk_read"], up("qk_read", step))
                                dve.wait_ge(g["sx_psum"], up("sx_psum", step))
                                nc.vector.tensor_tensor(qbd[:], bd_r[:], qf[:, 0:REG].unsqueeze(1).to_broadcast([128, H, REG]),
                                                        ALU.mult).then_inc(g["qbd_ready"], 1)
                            elif kind == "sim1":
                                dve.wait_ge(g["sim_dve"], up("sim_dve", step))
                                dve.wait_ge(g["sim_pool"], up("sim_pool", step))
                                for k, dst in enumerate((dots, nrm2)):
                                    nc.vector.tensor_reduce(dst[:], prod[:, k, :].rearrange("p (a d) -> p a d", d=HD),
                                                            AX.X, ALU.add).then_inc(g["sim_dve"], 1)
                            elif kind == "sim2":
                                steps = Steps(dve, g["sim_dve"], up("sim_dve", step))
                                steps.settle()
                                steps.done(nc.vector.tensor_scalar(rs[:].bitcast(I32), nrm2[:].bitcast(I32), -0.5, RSQRT_BITS,
                                                                   ALU.mult, ALU.add))
                                steps.settle()
                                for _ in range(3):
                                    steps.done(nc.vector.tensor_tensor(rs2[:], rs[:], rs[:], ALU.mult))
                                    steps.settle()
                                    steps.done(nc.vector.scalar_tensor_tensor(rs2[:], rs2[:], -0.5, nrm2[:], ALU.mult, ALU.mult))
                                    steps.settle()
                                    steps.done(nc.vector.scalar_tensor_tensor(rs[:], rs2[:], 1.5, rs[:], ALU.add, ALU.mult))
                                    steps.settle()
                                steps.done(nc.vector.tensor_tensor(dots[:], dots[:], rs[:], ALU.mult))
                                steps.settle()
                                apart(dve)
                                steps.done(nc.vector.tensor_reduce(sim[:, batch, :], dots[:].rearrange("p (j h) -> p j h", h=H),
                                                                   AX.X, ALU.add))

                    go(dve, part_work)

                @block.gpsimd
                def _(pool):
                    def raise_half(t, name):
                        nc.gpsimd.tensor_tensor(t[:], t[:], mhalf[:, 0:t.shape[1]], ALU.pow).then_inc(g[name], 1)

                    def part_work(part):
                        up, thru = part.upto, part.through
                        for step in part.steps:
                            kind, m, kb = step.kind, step.m, step.kb
                            batch = 2 * part.turn + step.batch
                            if kind == "ST" and counts(step, causal)["tri_done"]:
                                pool.wait_ge(g["exp_done"], thru("exp_done", step))
                                apart(pool)
                                diag = E[:, kb, :, 0:128]
                                nc.gpsimd.affine_select(out=diag, in_=diag, compare_op=ALU.is_ge, fill=0.0, base=0,
                                                        pattern=[[0, 4], [1, 128]], channel_multiplier=-1
                                                        ).then_inc(g["tri_done"], 1)
                            elif kind == "S" and counts(step, causal)["split"]:
                                steps = Steps(pool, g["split_step"], up("split_step", step))
                                pool.wait_ge(g["max_done"], thru("max_done", step))
                                pool.wait_ge(g["mT_psum"], up("mT_psum", step) - 1)
                                apart(pool)
                                n4, r4 = nm[:, m % 2], nmr[:, m % 2]
                                part3 = [nms[:, m % 2, :, 4 * t:4 * t + 4] for t in range(3)]
                                steps.done(nc.gpsimd.tensor_copy(part3[0], n4))
                                steps.settle()
                                steps.done(nc.gpsimd.tensor_tensor(r4, n4, part3[0], ALU.subtract))
                                steps.settle()
                                apart(pool)
                                steps.done(nc.gpsimd.tensor_copy(part3[1], r4))
                                steps.settle()
                                steps.done(nc.gpsimd.tensor_tensor(r4, r4, part3[1], ALU.subtract))
                                steps.settle()
                                apart(pool)
                                nc.gpsimd.tensor_copy(part3[2], r4).then_inc(g["split"], 1)
                            elif kind == "lay":
                                par = step.batch % 2
                                pool.wait_ge(g["pv_done"], up("pv_done", step))
                                pool.wait_ge(g["tok_read"], up("tok_read", step))
                                apart(pool)
                                nc.gpsimd.tensor_copy(vpad[:, par, :, :, 0:HD].rearrange("p k h d -> p (k h) d"),
                                                      v_all[:, batch, :, :].rearrange("p k (h d) -> p (k h) d", d=HD)
                                                      ).then_inc(g["v_ready%d" % par], 1)
                            elif kind in ("y", "xn_stats"):
                                pool.wait_ge(g["dve_step"], thru("dve_step", step))
                                raise_half(rstd, "pow_done")
                            elif kind.startswith("split"):
                                k, n = divmod(int(kind[5:]), 3)
                                src = (qf, kf)[k]
                                pool.wait_ge(g["qk_read"], up("qk_read", step))
                                pool.wait_ge(g["part_done"], up("part_done", step))
                                if n == 0:
                                    nc.gpsimd.tensor_tensor(res[:], src[:], parts[:, k, 1, :], ALU.subtract
                                                            ).then_inc(g["part_done"], 1)
                                elif n == 1:
                                    apart(pool)
                                    nc.gpsimd.tensor_copy(parts[:, k, 0, :], res[:]).then_inc(g["part_done"], 1)
                                else:
                                    nc.gpsimd.tensor_tensor(parts[:, k, 2, :], res[:], parts[:, k, 0, :], ALU.subtract
                                                            ).then_inc(g["part_done"], 1)
                            elif kind == "sim0":
                                pool.wait_ge(g["tok_read"], up("tok_read", step))
                                pool.wait_ge(g["sim_dve"], up("sim_dve", step))
                                nc.gpsimd.tensor_tensor(prod[:, 0, :].rearrange("p (j d) -> p j d", d=D),
                                                        qtok[:].rearrange("p (j d) -> p j d", d=D),
                                                        g_bc[:].unsqueeze(1).to_broadcast([128, NB, D]), ALU.mult
                                                        ).then_inc(g["sim_pool"], 1)
                                nc.gpsimd.tensor_tensor(prod[:, 1, :], qtok[:], qtok[:], ALU.mult).then_inc(g["sim_pool"], 1)

                    go(pool, part_work)

                @block.sync
                def _(sp):
                    def part_work(part):
                        up, thru = part.upto, part.through
                        for step in part.steps:
                            kind, m = step.kind, step.m
                            batch = 2 * part.turn + step.batch
                            if kind == "load":
                                par = step.batch % 2
                                there = g["qk_load%d" % par]
                                sp.wait_ge(g["st_ready"], up("st_ready", step))
                                apart(sp)
                                if causal:
                                    sp.wait_ge(g["stored"], up("stored", step))
                                    apart(sp)
                                for j in range(2):
                                    sp.dma_start(qpad[48 * j:48 * j + 48, par, :, 2 * j:2 * j + 2, :].rearrange("r c g s -> r c (g s)"),
                                                 q_scr[causal][batch, j].rearrange("t (d c p) s -> (t d) c (p s)", d=HD, c=QUADS)
                                                 ).then_inc(there, 16)
                                sp.dma_start(kk[0:96, par, :],
                                             k_scr[causal][batch].rearrange("j t (d p) s -> (j t d) (p s)", d=HD)).then_inc(there, 16)
                                if not causal:
                                    sp.dma_start(qpad[96:98, par].rearrange("r c g s -> r (c g) s"),
                                                 m_scr[0:2, batch, :].unsqueeze(1).to_broadcast([2, H, S])).then_inc(there, 16)
                                    sp.dma_start(kk[96:98, par].rearrange("r (p s) -> r p s", s=S),
                                                 m_scr[2:4, batch, :].unsqueeze(1).to_broadcast([2, PAIRS, S])).then_inc(there, 16)
                            elif kind == "mT":
                                sp.wait_ge(g["mT_ready"], thru("mT_ready", step))
                                apart(sp)
                                sp.dma_start(qpad[MAX_ROW:ROWS, (m // 4) % 2, m % 4], mT[:, m % 2, :]
                                             ).then_inc(g["max_row%d" % (m % 2)], 16)
                            elif kind in ("split2", "split5"):
                                s = 0 if kind == "split2" else 1
                                terms, scr = ((Q_TERMS, q_scr), (K_TERMS, k_scr))[s]
                                sp.wait_ge(g["part_done"], thru("part_done", step))
                                apart(sp)
                                for t, p in enumerate(terms):
                                    sp.dma_start(scr[not step.two][batch, :, t, :, :], parts[:, s, p, :]).then_inc(g["stored"], 16)
                            elif kind == "x_new" and not causal:
                                sp.wait_ge(g["x_done"], thru("x_done", step))
                                apart(sp)
                                sp.dma_start(out[batch].rearrange("(j p) d -> p j d", p=128), x_all[:, batch, :, :]
                                             ).then_inc(g["out_done"], 16)

                    go(sp, part_work)
                    for name in ("stored", "out_done"):
                        if after.after()[name]:
                            sp.wait_ge(g[name], START + after.after()[name])

        CSTEPS = 19

        def class_stage():
            cols = sb("cols", [128, 8])
            big = sb("big", [128, 2, B, NB])
            cls = sb("cls", [128, 3, B, NB])
            rows4 = sb("rows4", [128, 5, B, NB], BF16)
            rowsT = sb("rowsT", [B * NB, 5, 128], BF16)
            ext = sx_all[:]
            penb = E[0:XQ, 2].rearrange("p g s -> p (g s)").bitcast(BF16)
            xm = sb("xm", [XQ, B])
            xsum = sb("xsum", [XQ, B])
            eT = sb("eT", [128, NB, XQ])
            w80 = sb("w80", [XQ, D])
            c_step, red, rT_psum, rT_read = sem("d_step"), sem("d_red"), sem("d_rT_psum"), sem("d_rT_read")
            stored, pen_in, x_step = sem("d_stored"), sem("d_pen_in"), sem("d_x_step")
            xe, xT_, xTr, xo, xw, x5, x5r = (sem("d_x%d" % n) for n in range(7))
            ps_r = work[:, 0, :].bitcast(BF16)

            with nc.Block() as block:
                @block.gpsimd
                def _(pool):
                    nc.gpsimd.memset(cols[:, 0:1], 1.0).then_inc(red, 1)
                    pool.wait_ge(red, 1)
                    apart(pool)
                    nc.gpsimd.affine_select(out=cols[:, 0:1], in_=cols[:, 0:1], compare_op=ALU.is_ge, fill=0.0, base=REG - 1,
                                            pattern=[[0, 1]], channel_multiplier=-1).then_inc(red, 1)
                    pool.wait_ge(c_step, 5)
                    nc.gpsimd.partition_all_reduce(cols[:, 4:6], cols[:, 2:4], 128,
                                                   bass.bass_isa.ReduceOp.max).then_inc(red, 1)

                @block.vector
                def _(dve):
                    s = Steps(dve, c_step)
                    dve.wait_ge(red, 2)
                    s.done(nc.vector.tensor_copy(big[:, 0], sim[:]))
                    s.done(nc.vector.tensor_scalar(big[:, 1], sim[:], -1.0, None, ALU.mult))
                    s.settle()
                    s.done(nc.vector.tensor_scalar(cols[:, 1:2], cols[:, 0:1], -BIG, None, ALU.mult))
                    s.settle()
                    s.done(nc.vector.tensor_scalar(big[:, :, :, 0], big[:, :, :, 0], cols[:, 1:2], None, ALU.add))
                    s.settle()
                    s.done(nc.vector.tensor_reduce(cols[:, 2:4], big[:].rearrange("p a b j -> p a (b j)"), AX.X, ALU.max))
                    dve.wait_ge(red, 3)
                    s.done(nc.vector.tensor_tensor(cols[:, 6:7], cols[:, 4:5], cols[:, 5:6], ALU.add))
                    s.settle()
                    flat = sim[:]
                    s.done(nc.vector.tensor_scalar(cls[:, 0], flat, cols[:, 5:6], None, ALU.add))
                    s.done(nc.vector.reciprocal(cols[:, 6:7], cols[:, 6:7]))
                    s.settle()
                    s.done(nc.vector.tensor_scalar(cls[:, 0], cls[:, 0], cols[:, 6:7], 0.9, ALU.mult, ALU.is_gt))
                    s.settle()
                    s.done(nc.vector.tensor_copy(cls[:, 2], cls[:, 0]))
                    s.settle()
                    s.done(nc.vector.tensor_scalar(cls[:, 0, :, 0], cls[:, 0, :, 0], cols[:, 0:1], None, ALU.max))
                    s.settle()
                    s.done(nc.vector.tensor_scalar(cls[:, 1], cls[:, 0], -1.0, 1.0, ALU.mult, ALU.add))
                    s.done(nc.vector.tensor_scalar(cols[:, 7:8], cols[:, 0:1], -1.0, 1.0, ALU.mult, ALU.add))
                    s.settle()
                    s.done(nc.vector.tensor_scalar(cls[:, 2, :, 0], cls[:, 2, :, 0], cols[:, 7:8], None, ALU.mult))
                    s.settle()
                    s.done(nc.vector.tensor_scalar(rows4[:, 0], cls[:, 1], -BIG, None, ALU.mult))
                    s.done(nc.vector.tensor_scalar(rows4[:, 1], cls[:, 0], -BIG, None, ALU.mult))
                    s.done(nc.vector.tensor_copy(rows4[:, 2], cls[:, 2]))
                    s.done(nc.vector.tensor_copy(rows4[:, 3], cls[:, 1]))
                    s.done(nc.vector.tensor_scalar(rows4[:, 4], cls[:, 2], -BIG, None, ALU.mult))
                    s.settle()
                    assert s.n == CSTEPS, s.n
                    dve.wait_ge(rT_psum, 1)
                    nc.vector.tensor_copy(rowsT[:].rearrange("p k t -> p (k t)"), ps_r[0:B * NB, 0:640]).then_inc(rT_read, 1)

                    dve.wait_ge(pen_in, 16)
                    xs = Steps(dve, x_step)
                    xs.done(nc.vector.tensor_tensor(ext.rearrange("p b s -> p (b s)"), sx_all[:].rearrange("p b s -> p (b s)"),
                                                    penb, ALU.add))
                    xs.settle()
                    xs.done(nc.vector.tensor_reduce(xm[:], ext, AX.X, ALU.max, negate=True))
                    xs.settle()
                    xs.done(nc.vector.tensor_scalar(xm[:], xm[:], SCALE, None, ALU.mult))
                    for b in range(B):
                        dve.wait_ge(xT_, b + 1)
                        if b:
                            dve.wait_ge(xo, b)
                        nc.vector.tensor_copy(eT[:].rearrange("p k q -> p (k q)"), work[:, 1, 0:NB * XQ]).then_inc(xTr, 1)
                        if b == 0:
                            dve.wait_ge(xe, B)
                            xs.done(nc.vector.reciprocal(xsum[:], xsum[:]))
                            xs.settle()
                        dve.wait_ge(xo, b + 1)
                        if b:
                            dve.wait_ge(x5, b)
                        nc.vector.scalar_tensor_tensor(out=w80[:], in0=work[0:XQ, 2, 0:D], scalar=xsum[:, b:b + 1],
                                                       in1=bd_c[:], op0=ALU.mult, op1=ALU.mult).then_inc(xw, 1)
                        dve.wait_ge(x5, b + 1)
                        nc.vector.tensor_copy(o_neg[:, b, :], pv[0:REG, 0:D]).then_inc(x5r, 1)

                @block.scalar
                def _(act):
                    act.wait_ge(x_step, 3)
                    for b in range(B):
                        nc.scalar.activation(ext[:, b, :], ext[:, b, :], ACT.Exp, scale=SCALE, bias=xm[:, b:b + 1],
                                             accum_out=xsum[:, b:b + 1]).then_inc(xe, 1)

                @block.tensor
                def _(pe):
                    pe.wait_ge(c_step, CSTEPS)
                    for k in range(5):
                        mm = nc.tensor.transpose(ps_r[0:B * NB, k * 128:(k + 1) * 128],
                                                 rows4[:, k].rearrange("p b j -> p (b j)"), id16[:])
                    mm.then_inc(rT_psum, 1)
                    for b in range(B):
                        pe.wait_ge(xe, b + 1)
                        if b:
                            pe.wait_ge(xTr, b)
                        for k in range(NB):
                            mm = nc.tensor.transpose(work[:, 1, k * XQ:(k + 1) * XQ], ext[:, b, k * 128:(k + 1) * 128],
                                                     id32[0:XQ, 0:XQ])
                        mm.then_inc(xT_, 1)
                        pe.wait_ge(xTr, b + 1)
                        if b:
                            pe.wait_ge(xw, b)
                        for k in range(NB):
                            mm = nc.tensor.matmul(work[0:XQ, 2, 0:D], eT[:, k, :], v_all[:, b, k, :],
                                                  start=(k == 0), stop=(k == NB - 1))
                        mm.then_inc(xo, 1)
                        pe.wait_ge(xw, b + 1)
                        if b:
                            pe.wait_ge(x5r, b)
                        nc.tensor.matmul(pv[0:REG, 0:D], selr_sb[:], w80[:], start=True, stop=True).then_inc(x5, 1)

                @block.sync
                def _(sp):
                    sp.wait_ge(rT_read, 1)
                    sp.dma_start(m_scr.rearrange("k b (j t) -> (b j) k t", t=128), rowsT[:]).then_inc(stored, 16)
                    sp.wait_ge(stored, 16)
                    sp.dma_start(penb, m_scr[4:5].rearrange("o b s -> o (b s)").to_broadcast([XQ, B * S])).then_inc(pen_in, 16)
                    sp.wait_ge(pen_in, 16)

        phase("p1_", True)
        class_stage()
        phase("p2_", False)


def kernel(**inputs):
    import ml_dtypes
    import numpy as np
    import concourse.bacc as bacc
    from concourse.bass_utils import run_bass_kernel_spmd as run

    a = {k: np.asarray(v) for k, v in inputs.items()}

    def pair_rows(w):
        return w.reshape((4, 2, 2, HD) + w.shape[1:]).transpose((1, 3, 0, 2) + tuple(range(4, 3 + w.ndim))).reshape(w.shape)

    w2 = a["L0_ffn_W_qkv"]
    head = pair_rows(np.repeat(np.arange(H), HD))
    cols = np.repeat(np.arange(H), REG)
    arrays = {
        "x": a["L0_attn_x"],
        "wqT": pair_rows(a["L0_attn_Wq"]).T, "wkT": pair_rows(a["L0_attn_Wk"]).T,
        "wvT": a["L0_attn_Wv"].T, "woT": a["L0_attn_Wo"].T,
        "bq": pair_rows(a["L0_attn_bq"])[:, None], "bk": pair_rows(a["L0_attn_bk"])[:, None],
        "bv": a["L0_attn_bv"][None, :], "bo": a["L0_attn_bo"][None, :],
        "g_info": a["L0_ffn_g_info"][0, 0:1, :],
        "w2q": np.concatenate([w2[:, 0:D], pair_rows(w2[:, 0:D].T).T], axis=1),
        "w2k": pair_rows(w2[:, D:2 * D].T).T, "w2v": w2[:, 2 * D:3 * D],
        "wpT": a["L0_ffn_W_proj"], "bp": a["L0_ffn_b_proj"][None, :],
        "ident": np.eye(128, dtype=np.float32),
        "tri": np.triu(np.full((128, 128), -BIG, dtype=np.float32), 1).astype(ml_dtypes.bfloat16),
        "bd_rows": (head[:, None] == cols[None, :]).astype(np.float32),
        "bd_cols": (cols[:, None] == np.repeat(np.arange(H), HD)[None, :]).astype(np.float32),
        "sel_r": (np.tile(np.arange(REG), H)[:, None] == np.arange(REG)[None, :]).astype(np.float32),
    }
    arrays = {k: np.ascontiguousarray(v) for k, v in arrays.items()}
    nc = bacc.Bacc("TRN2", target_bir_lowering=False, num_devices=1)
    aps = {k: nc.dram_tensor(k, v.shape, mybir.dt.from_np(v.dtype), kind="ExternalInput").ap() for k, v in arrays.items()}
    out = nc.dram_tensor("out", (B, S, D), F32, kind="ExternalOutput").ap()
    build(nc, out=out, **aps)
    r = run(nc, [arrays], core_ids=[0])
    return r.results[0]["out"]
```

```python
from contextlib import ExitStack

import concourse.bass as bass
from concourse import mybir

F32 = mybir.dt.float32
BF16 = mybir.dt.bfloat16
U32 = mybir.dt.uint32
I32 = mybir.dt.int32
ALU = mybir.AluOpType
ACT = mybir.ActivationFunctionType
AX = mybir.AxisListType

B, S, D, H, HD = 8, 512, 128, 16, 8
REG = 5
NB = S // 128
PAIRS, QUADS = H // 2, H // 4
TERMS = 6
MASK_ROW = 2 * TERMS * HD
MAX_ROW = MASK_ROW + 2
ROWS = MAX_ROW + 3
VW = 32
SCALE = 1.0 / float(HD) ** 0.5
BIG = 1.0e30
EPS = 1e-5
RSQRT_BITS = float(0x5f3759df)
XQ = H * REG
STEPS = 2 * QUADS
TURNS = B // 2
START = 16
TERMS_OF = (((0, 2), (1, 3, 4), (5,)), ((0, 3), (1, 2, 5), (4,)))


STORED_AT = (1, 0, 2)


class Steps:

    def __init__(self, eng, sem, base=0):
        self.eng, self.sem, self.base, self.n = eng, sem, base, 0

    def done(self, ins):
        ins.then_inc(self.sem, 1)
        self.n += 1

    def settle(self):
        self.eng.wait_ge(self.sem, self.base + self.n)


def score_uses(causal):
    if not causal:
        return [(i, [g], S) for i in range(NB) for g in range(4)]
    return ([(3, [g], 512) for g in range(4)] + [(2, [g], 384) for g in range(4)]
            + [(1, [0, 1], 256), (1, [2, 3], 256), (0, [0, 1, 2, 3], 128)])


def exp_uses(causal, kb):
    queries = S - 128 * kb if causal else S
    together = min(4, 512 // queries)
    return [(range(h, h + together), queries) for h in range(0, 4, together)]



SIM = ("sim_qg", "sim_qq", "sim_sums", "sim_root0", "sim_root1", "sim_root2")


def prepared(stats, norm, q, two):
    pieces = [("xn_stats0", stats), ("xn_stats1", stats + 1), ("xn0", norm[0]), ("xn1", norm[1]), ("xT", q - 1), ("q", q),
              ("k", q + 1)] + [("qbd", q + 1)] * two + [("tok", q + 2)]
    pieces += [("split%d" % n, q + 1 + n) for n in range(6)]
    return pieces + ([("sx", q + 3)] + [(k, q + 3 + n) for n, k in enumerate(SIM)]) * two


def posted(first):
    return [("reg", first), ("oT", first + 1), ("y", first + 2), ("y_stats0", first + 2), ("y_stats1", first + 3),
            ("x_new0", first + 5), ("x_new1", first + 6)]


SLOTS = 4 * STEPS
PREP1_EVEN = prepared(0, (3, 4), 6, False)
POST_ODD = posted(3)
PREP2_ODD = prepared(9, (12, 12), 14, True)
PREP1_ODD = prepared(13, (16, 17), 22, False)
POST_EVEN = posted(19)
PREP2_EVEN = prepared(25, (28, 28), 30, True)
NEG_EVEN = [("n_add", 9), ("n_max", 10), ("n_exp", 11), ("n_eT", 12), ("n_o", 13), ("n_sum", 14)]
NEG_ODD = [("n_add", 25), ("n_max", 26), ("n_exp", 27), ("n_eT", 28), ("n_o", 29), ("n_sum", 30)]
SPLITS = ["split%d" % n for n in (0, 3, 1, 4, 2, 5)]
LAST_ORDER = [(0, "tok"), (1, "reg"), (1, "oT")] + [(0, "split%d" % n) for n in range(6)] + [
    (0, "sx"), (1, "y"), (1, "y_stats0"), (1, "y_stats1"), (1, "x_new0"), (1, "x_new1"), (1, "xn_stats0"), (1, "xn_stats1"),
    (0, "sim_qg"), (0, "sim_qq"), (1, "xn0"), (1, "xn1"), (1, "xT")] + [(0, k) for k in SIM[2:]] + [
    (1, "tok"), (1, "q"), (1, "k"), (1, "sim_qg"), (1, "sim_qq")] + [(1, k) for k in SPLITS] + [
    (1, k) for k in SIM[2:]] + [(1, "qbd"), (1, "sx")]

SIGNALS = ("st_ready exp_done tri_done s_ready max_done split split_step mT_psum mT_ready max_row0 max_row1 "
           "pv_done pv_read oT_psum rec_done o_done qk_load0 qk_load1 qk_late0 qk_late1 v_ready0 v_ready1 "
           "dve_step pow_done xn_ready xT_psum xT_ready qk_psum qk_read tok_psum tok_read part_done0 part_done1 stored0 stored1 "
           "qbd_ready sx_psum sx_read sim_pool sim_dve post_psum post_read y_psum y_read x_done reg_step out_done "
           "n_step n_exp n_eT_psum n_eT_read n_o_psum n_o_read n_sum_psum n_sum_read").split()
RINGS = {"work": 4, "st": 3}
BANK_READ = {"ST": "exp_done", "S": "max_done", "mT": "mT_ready", "OT": "o_done", "xT": "xT_ready", "q": "qk_read",
             "k": "qk_read", "tok": "tok_read", "sx": "sx_read", "oT": "post_read", "y": "y_read", "n_eT": "n_eT_read", "n_o": "n_o_read",
             "n_sum": "n_sum_read"}


MAXIMA_AT = {False: [range(4 * kb, 4 * kb + 4) for kb in range(NB)],
             True: [range(0, 3), range(3, 6), range(6, 8), range(8, 11)]}


class Step:

    def __init__(self, kind, m=0, kb=0, batch=0, two=False, use=0):
        self.kind, self.m, self.kb, self.batch, self.two, self.use = kind, m, kb, batch, two, use


def work_of(pieces, batch, two, slot=None):
    return [Step(k, batch=batch, two=two) for k, at in pieces if slot is None or at == slot]


def turn_steps(causal, first, last):
    steps = []
    load_at = {2 if causal and first else 0: 1, 16: 2}
    for m in range(STEPS):
        for kb in range(NB):
            slot = 4 * m + kb
            load = [Step(k, batch=load_at[slot]) for k in ("load", "lay")
                    ] if slot in load_at and not (last and load_at[slot] == 2) else []
            steps += load[0:1]
            others = [Step("ST", m, kb, use=n) for n in range(len(exp_uses(causal, kb)))]
            if slot > 0 or not first:
                others.append(Step("PV", (slot - 1) // 4, (kb - 1) % 4))
            maxima = [] if last and m + 2 >= STEPS else [Step("S", m + 2, use=n) for n in MAXIMA_AT[causal][kb]]
            placed = [(n / len(maxima), 0, n) for n in range(len(maxima))] + [((n + 0.5) / len(others), 1, n)
                                                                             for n in range(len(others))]
            steps += [(maxima, others)[which][n] for _, which, n in sorted(placed)]
            steps += load[1:2]
            if kb == 1 and not (last and m + 1 == STEPS):
                steps.append(Step("mT", m + 1))
            if kb == 2 and (m > 0 or not first):
                steps.append(Step("OT", m - 1))
            if causal and not first:
                steps += work_of(PREP2_EVEN, -2, True, slot + SLOTS)
            if causal and not last:
                steps += work_of(PREP1_EVEN, 2, False, slot)
            if not first:
                steps += work_of(POST_ODD, -1, True, slot) + (work_of(PREP2_ODD, -1, True, slot) if causal else [])
            if causal and not last:
                steps += work_of(PREP1_ODD, 3, False, slot)
            if not causal:
                steps += work_of(NEG_EVEN, 0, True, slot) + work_of(NEG_ODD, 1, True, slot)
            steps += work_of(POST_EVEN, 0, True, slot) + (work_of(PREP2_EVEN, 0, True, slot) if causal else [])
    return steps


def ahead_steps(causal):
    steps = []
    if causal:
        steps = [Step(k) for k, _ in PREP1_EVEN if k not in SPLITS] + [Step(k) for k in SPLITS]
    steps += [Step("load", batch=0), Step("lay", batch=0)]
    steps += work_of([(k, at) for k, at in PREP1_ODD if at < 22], 1, False) if causal else []
    between = work_of([(k, at) for k, at in PREP1_ODD if at >= 22], 1, False) if causal else []
    n_uses = len(score_uses(causal))
    for n in range(2 * n_uses):
        steps.append(Step("S", n // n_uses, use=n % n_uses))
        steps += between[n // 2:n // 2 + 1] if n % 2 == 0 else []
        if n == n_uses + 3:
            steps.append(Step("mT", 0))
    return steps


def after_steps(causal):
    steps = [Step("PV", -1, NB - 1), Step("OT", -1)]
    if not causal:
        return steps + work_of(POST_ODD, 1, True)
    left = [k for k, at in PREP2_EVEN if at >= SLOTS]
    return steps + [Step(k, batch=b, two=True) for b, k in LAST_ORDER if b or k in left]


def counts(step, causal):
    k, two = step.kind, step.two
    if k == "ST":
        return {"st_ready": 1, "exp_done": 1, "tri_done": int(causal and step.use == len(exp_uses(causal, step.kb)) - 1)}
    if k == "S":
        over = int(step.use == len(score_uses(causal)) - 1)
        return {"s_ready": 1, "max_done": 1, "split": over, "split_step": 4 * over}
    if k == "PV":
        return {"pv_done": 1, "pv_read": int(step.kb == 3)}
    if k == "mT":
        return {"mT_psum": 1, "mT_ready": 1, "max_row%d" % (step.m % 2): 16}
    if k.startswith("split"):
        n = int(k[5:])
        return {"part_done%d" % (n // 3): 1, "stored%d" % (n // 3): 16 * len(TERMS_OF[n // 3][STORED_AT[n % 3]])}
    return {
        "OT": {"oT_psum": 1, "rec_done": 1, "o_done": 1},
        "load": {"qk_load%d" % (step.batch % 2): 16 * (3 if causal else 5),
                 "qk_late%d" % (step.batch % 2): 16 * (3 if causal else 4)},
        "lay": {"v_ready%d" % (step.batch % 2): 1},
        "xn_stats0": {"dve_step": NB},
        "xn_stats1": {"dve_step": NB + 1, "pow_done": 1},
        "xn0": {"xn_ready": NB // 2},
        "xn1": {"xn_ready": NB // 2},
        "xT": {"xT_psum": 1, "xT_ready": 1},
        "q": {"qk_psum": 1, "qk_read": 2},
        "k": {"qk_psum": 1, "qk_read": 2},
        "tok": {"tok_psum": 1 + two, "tok_read": 1 + two},
        "qbd": {"qbd_ready": 1},
        "sx": {"sx_psum": 1, "sx_read": 1},
        "sim_qg": {"sim_pool": 1},
        "sim_qq": {"sim_pool": 1},
        "sim_sums": {"sim_dve": 2},
        "sim_root0": {"sim_dve": 4},
        "sim_root1": {"sim_dve": 3},
        "sim_root2": {"sim_dve": 5},
        "n_add": {"n_step": 1},
        "n_max": {"n_step": 2},
        "n_exp": {"n_exp": 1},
        "n_eT": {"n_eT_psum": 1, "n_eT_read": 1, "n_step": 1},
        "n_o": {"n_o_psum": 1, "n_o_read": 1},
        "n_sum": {"n_sum_psum": 1, "n_sum_read": 1},
        "reg": {} if causal else {"reg_step": 2},
        "oT": {"post_psum": 1, "post_read": 1},
        "y": {"y_psum": 1, "y_read": 1},
        "y_stats0": {"dve_step": NB},
        "y_stats1": {"dve_step": NB + 1, "pow_done": 1},
        "x_new0": {"dve_step": NB // 2},
        "x_new1": {"dve_step": NB // 2, "x_done": 1, "out_done": 0 if causal else 16},
    }[k]


def banks_of(step, causal):
    k = step.kind
    return 1 + step.two if k == "tok" else int(k in BANK_READ)


class Part:

    def __init__(self, steps, causal, before, rings, tails=()):
        self.tails = tails
        self.steps, self.start, self.causal = steps, before, causal
        self.before, self.banks, self.by = [], [], {}
        local, rings = dict.fromkeys(SIGNALS, 0), dict(rings)
        for n, step in enumerate(steps):
            self.before.append(dict(local))
            for name, k in counts(step, causal).items():
                local[name] += k
            used = banks_of(step, causal)
            ring = "st" if step.kind == "ST" else "work"
            self.banks.append([(rings[ring] + b) % RINGS[ring] for b in range(used)])
            rings[ring] += used
            step.n = n
            self.by[step.kind, step.m, step.kb] = step
        self.total = local
        self.rings = rings

    def after(self):
        return {k: self.start[k] + self.total[k] for k in SIGNALS}

    def last_reads(self):
        reads = {}
        for step, banks in zip(self.steps, self.banks):
            for k, w in enumerate(banks):
                name = BANK_READ[step.kind]
                reads["st" if step.kind == "ST" else "work", w] = (name, self.total[name] - (self.before[step.n][name] + k + 1))
        return reads

    def at(self, turn, looped=0):
        self.turn, self.looped = turn, looped
        return self

    def upto(self, name, step):
        v = START + self.start[name] + self.before[step.n][name]
        if self.looped and self.total[name]:
            v = (self.turn - self.looped) * self.total[name] + v
        return v

    def through(self, name, step):
        return self.upto(name, step) + counts(step, self.causal).get(name, 0)


def build(nc, x, near, rows, tri, far, reg_tables, out):
    with ExitStack() as ctx:
        def sb(name, shape, dt=F32):
            return ctx.enter_context(nc.sbuf_tensor(name, shape, dt))

        def sem(name):
            return ctx.enter_context(nc.semaphore(name))

        def dram(name, shape, dt):
            return nc.dram_tensor(name, shape, dt).ap()

        x_all = sb("x_all", [128, B, NB, D])
        v_all = sb("v_all", [128, B, NB, D])
        o_turn = sb("o_turn", [128, 2, NB, D])
        qpad = sb("qpad", [128, 2, QUADS, 4, S], BF16)
        kk = sb("kk", [128, 2, PAIRS * S], BF16)
        vpad = sb("vpad", [128, 2, NB, H, VW])
        E = sb("E", [128, 4, 4, S])
        near_sb = sb("near_sb", [128, 4 * D + 2])
        wq_sb, wk_sb, wqv_sb, id32 = (near_sb[:, n * D:(n + 1) * D] for n in range(4))
        bq_sb, bk_sb = near_sb[:, 4 * D:4 * D + 1], near_sb[:, 4 * D + 1:4 * D + 2]
        rows_sb = sb("rows_sb", [128, 4, D])
        bv_bc, bo_bc, bp_bc, g_bc = (rows_sb[:, n, :] for n in range(4))
        far_sb = sb("far_sb", [128, 6 * D + H * REG])
        wo_sb, w2q_sb, w2k_sb = (far_sb[:, n * D:(n + 1) * D] for n in range(3))
        w2v_sb, wp_sb = far_sb[:, 3 * D:5 * D], far_sb[:, 5 * D:6 * D]
        bd_r = far_sb[:, 6 * D:].rearrange("p (h r) -> p h r", r=REG)
        reg_sb = sb("reg_sb", [XQ, D + REG])
        bd_c, selr_sb = reg_sb[:, 0:D], reg_sb[:, D:D + REG]
        id16 = sb("id16", [128, 128], BF16)
        tri_sb = sb("tri_sb", [128, 128], BF16)
        g_n = sb("g_n", [128, H])
        mhalf = sb("mhalf", [128, H])
        sim = sb("sim", [128, B, NB])
        sx_all = sb("sx_all", [XQ, B, S])
        o_neg = sb("o_neg", [REG, 2, D])
        xn = sb("xn", [128, NB, D])
        xT = sb("xT", [128, S])
        qf = sb("qf", [128, S])
        kf = sb("kf", [128, S])
        res = sb("res", [128, 2, S])
        parts = sb("parts", [128, 2, 3, S], BF16)
        stats = sb("stats", [128, NB, 6])
        mv = sb("mv", [128, NB, 2])
        rstd = sb("rstd", [128, NB])
        y_sb = sb("y_sb", [128, NB, D])
        oT2 = sb("oT2", [128, S])
        qtok = sb("qtok", [128, NB * D])
        prod = sb("prod", [128, 2, NB * D])
        dots = sb("dots", [128, NB * H])
        nrm2 = sb("nrm2", [128, NB * H])
        rs = sb("rs", [128, NB * H])
        rs2 = sb("rs2", [128, NB * H])
        qbd = sb("qbd", [128, H, REG])
        pen = sb("pen", [XQ, 2, S], BF16)
        ext = sb("ext", [XQ, S])
        xm = sb("xm", [XQ, 1])
        xsum = sb("xsum", [XQ, 1])
        eT = sb("eT", [128, NB * XQ])
        w80 = sb("w80", [XQ, D])
        nm = sb("nm", [128, 2, NB, 4])
        nmr = sb("nmr", [128, 2, NB, 4])
        nms = sb("nms", [128, 2, NB, 12], BF16)
        mT = sb("mT", [12, 2, S], BF16)
        oT = sb("oT", [128, 2, S])
        rec = sb("rec", [128, NB, 4])

        work = ctx.enter_context(nc.psum_tensor("work", [128, RINGS["work"], 512], F32))
        st = ctx.enter_context(nc.psum_tensor("st", [128, RINGS["st"], 512], F32))
        pv = ctx.enter_context(nc.psum_tensor("pv", [128, 512], F32))

        q_scr = {c: dram("q_scr%d" % c, [B, 2, TERMS, 64, S], BF16) for c in (True, False)}
        k_scr = {c: dram("k_scr%d" % c, [B, 2, TERMS, 64, S], BF16) for c in (True, False)}
        m_scr = dram("m_scr", [5, B, S], BF16)

        signal = {tag + name: sem(tag + name) for tag in ("p1_", "p2_") for name in SIGNALS}

        loaded, loaded_late = sem("loaded"), sem("loaded_late")
        held = sem("held")
        cleared, halves, v_zero, k_ones = sem("cleared"), sem("halves"), sem("v_zero"), sem("k_ones")
        g_step = sem("g_step")
        n_late = 1 + 1 + (B - 2)
        with nc.Block() as block:
            @block.sync
            def _(sp):
                def x_load(b):
                    return x_all[:, b, :, :], x[b].rearrange("(j p) d -> p j d", p=128)

                loads = [x_load(0), (near_sb[:], near), (rows_sb[:].rearrange("p a d -> p (a d)"),
                                                         rows.to_broadcast([128, 4 * D])), x_load(1), (tri_sb[:], tri)]
                for dst, src in loads:
                    sp.dma_start(dst, src).then_inc(loaded, 16)
                for dst, src in [(far_sb[:], far), (reg_sb[:], reg_tables)] + [x_load(b) for b in range(2, B)]:
                    sp.dma_start(dst, src).then_inc(loaded_late, 16)
                for name in SIGNALS:
                    sp.sem_inc(signal["p1_" + name], START)
                sp.wait_ge(loaded, 16 * len(loads))

            @block.scalar
            def _(act):
                for name in SIGNALS:
                    act.sem_inc(signal["p2_" + name], START)

            @block.vector
            def _(dve):
                nc.vector.memset(qpad[:], 0.0).then_inc(cleared, 1)
                dve.wait_ge(loaded, 16 * 5)
                nc.vector.tensor_copy(id16[:], id32).then_inc(cleared, 1)

            @block.gpsimd
            def _(pool):
                nc.gpsimd.memset(kk[MASK_ROW:ROWS].bitcast(U32), 0x3f803f80).then_inc(k_ones, 1)
                pool.wait_ge(k_ones, 1)
                nc.gpsimd.memset(mhalf[:], -0.5).then_inc(halves, 1)
                nc.gpsimd.memset(vpad[:], 0.0).then_inc(v_zero, 1)
                pool.wait_ge(v_zero, 1)
                nc.gpsimd.memset(vpad[:, :, :, :, HD:HD + 1].rearrange("p a k h o -> p (a k h) o"), 1.0).then_inc(cleared, 1)

        def apart(eng):
            eng.sem_inc(held, 1)

        CSTEPS = 19
        cols = sb("cols", [128, 8])
        big = sb("big", [128, 2, B, NB])
        cls = sb("cls", [128, 3, B, NB])
        rows4 = sb("rows4", [128, 5, B, NB], BF16)
        rowsT = sb("rowsT", [B * NB, 5, 128], BF16)
        c_step, red, rT_psum, rT_read = sem("d_step"), sem("d_red"), sem("d_rT_psum"), sem("d_rT_read")
        m_stored = sem("d_stored")
        ps_r = pv[:].bitcast(BF16)

        def class_rows_first(pool):
            nc.gpsimd.memset(cols[:, 0:1], 1.0).then_inc(red, 1)
            pool.wait_ge(red, 1)
            apart(pool)
            nc.gpsimd.affine_select(out=cols[:, 0:1], in_=cols[:, 0:1], compare_op=ALU.is_ge, fill=0.0, base=REG - 1,
                                    pattern=[[0, 1]], channel_multiplier=-1).then_inc(red, 1)

        def class_rows_gpsimd(pool):
            pool.wait_ge(c_step, 5)
            nc.gpsimd.partition_all_reduce(cols[:, 4:6], cols[:, 2:4], 128,
                                           bass.bass_isa.ReduceOp.max).then_inc(red, 1)

        def class_rows_vector(dve):
            s = Steps(dve, c_step)
            dve.wait_ge(red, 2)
            dve.wait_ge(signal["p1_sim_dve"], START + B * 14)
            s.done(nc.vector.tensor_copy(big[:, 0], sim[:]))
            s.done(nc.vector.tensor_scalar(big[:, 1], sim[:], -1.0, None, ALU.mult))
            s.settle()
            s.done(nc.vector.tensor_scalar(cols[:, 1:2], cols[:, 0:1], -BIG, None, ALU.mult))
            s.settle()
            s.done(nc.vector.tensor_scalar(big[:, :, :, 0], big[:, :, :, 0], cols[:, 1:2], None, ALU.add))
            s.settle()
            s.done(nc.vector.tensor_reduce(cols[:, 2:4], big[:].rearrange("p a b j -> p a (b j)"), AX.X, ALU.max))
            dve.wait_ge(red, 3)
            s.done(nc.vector.tensor_tensor(cols[:, 6:7], cols[:, 4:5], cols[:, 5:6], ALU.add))
            s.settle()
            flat = sim[:]
            s.done(nc.vector.tensor_scalar(cls[:, 0], flat, cols[:, 5:6], None, ALU.add))
            s.done(nc.vector.reciprocal(cols[:, 6:7], cols[:, 6:7]))
            s.settle()
            s.done(nc.vector.tensor_scalar(cls[:, 0], cls[:, 0], cols[:, 6:7], 0.9, ALU.mult, ALU.is_gt))
            s.settle()
            s.done(nc.vector.tensor_copy(cls[:, 2], cls[:, 0]))
            s.settle()
            s.done(nc.vector.tensor_scalar(cls[:, 0, :, 0], cls[:, 0, :, 0], cols[:, 0:1], None, ALU.max))
            s.settle()
            s.done(nc.vector.tensor_scalar(cls[:, 1], cls[:, 0], -1.0, 1.0, ALU.mult, ALU.add))
            s.done(nc.vector.tensor_scalar(cols[:, 7:8], cols[:, 0:1], -1.0, 1.0, ALU.mult, ALU.add))
            s.settle()
            s.done(nc.vector.tensor_scalar(cls[:, 2, :, 0], cls[:, 2, :, 0], cols[:, 7:8], None, ALU.mult))
            s.settle()
            s.done(nc.vector.tensor_scalar(rows4[:, 0], cls[:, 1], -BIG, None, ALU.mult))
            s.done(nc.vector.tensor_scalar(rows4[:, 1], cls[:, 0], -BIG, None, ALU.mult))
            s.done(nc.vector.tensor_copy(rows4[:, 2], cls[:, 2]))
            s.done(nc.vector.tensor_copy(rows4[:, 3], cls[:, 1]))
            s.done(nc.vector.tensor_scalar(rows4[:, 4], cls[:, 2], -BIG, None, ALU.mult))
            s.settle()
            assert s.n == CSTEPS, s.n
            dve.wait_ge(rT_psum, 1)
            nc.vector.tensor_copy(rowsT[:].rearrange("p k t -> p (k t)"), ps_r[0:B * NB, 0:640]).then_inc(rT_read, 1)


        def class_rows_tensor(pe):
            pe.wait_ge(c_step, CSTEPS)
            for k in range(5):
                mm = nc.tensor.transpose(ps_r[0:B * NB, k * 128:(k + 1) * 128],
                                         rows4[:, k].rearrange("p b j -> p (b j)"), id16[:])
            mm.then_inc(rT_psum, 1)

        def class_rows_sync(sp):
            sp.wait_ge(rT_read, 1)
            sp.dma_start(m_scr.rearrange("k b (j t) -> (b j) k t", t=128), rowsT[:]).then_inc(m_stored, 16)
            sp.wait_ge(m_stored, 16)

        def load_rows(sp, causal, batch, par, half, there):
            quads = slice(2 * half, 2 * half + 2)
            for j in range(2):
                sp.dma_start(qpad[48 * j:48 * j + 48, par, quads, 2 * j:2 * j + 2, :].rearrange("r c g s -> r c (g s)"),
                             q_scr[causal][batch, j].rearrange("t (d c p) s -> (t d) c (p s)", d=HD, c=QUADS)[:, quads]
                             ).then_inc(there, 16)
            keys = slice(4 * half * S, 4 * (half + 1) * S)
            sp.dma_start(kk[0:96, par, keys],
                         k_scr[causal][batch].rearrange("j t (d p) s -> (j t d) (p s)", d=HD)[:, keys]).then_inc(there, 16)

        def phase(tag, causal):
            g = {name: signal[tag + name] for name in SIGNALS}
            post_w, post_b = (wo_sb, bo_bc) if causal else (wp_sb, bp_bc)

            zero = dict.fromkeys(SIGNALS, 0)
            ahead = Part(ahead_steps(causal), causal, zero, dict.fromkeys(RINGS, 0))
            first = Part(turn_steps(causal, True, False), causal, ahead.after(), ahead.rings, [ahead])
            middle = Part(turn_steps(causal, False, False), causal, first.after(), first.rings, [first])
            middle.tails.append(middle)
            middle_end = {k: middle.start[k] + (TURNS - 2) * middle.total[k] for k in SIGNALS}
            last = Part(turn_steps(causal, False, True), causal, middle_end, first.rings, [middle])
            after = Part(after_steps(causal), causal, last.after(), last.rings, [last])

            def go(eng, part_work, between=None):
                part_work(ahead.at(0))
                if causal:
                    eng.wait_ge(loaded_late, 16 * n_late)
                    if between:
                        between()
                part_work(first.at(0))
                with eng.Fori(1, TURNS - 1) as turn:
                    part_work(middle.at(turn, 1))
                part_work(last.at(TURNS - 1))
                part_work(after.at(TURNS - 1))

            with nc.Block() as block:
                @block.tensor
                def _(pe):
                    def part_work(part):
                        up, thru = part.upto, part.through
                        holder = {(ring, w): [] for ring in RINGS for w in range(RINGS[ring])}
                        for before in part.tails:
                            for bank, (name, rise) in before.last_reads().items():
                                holder[bank].append((g[name], up(name, part.steps[0]) - rise))

                        def take(step, k):
                            w = part.banks[step.n][k]
                            ring = "st" if step.kind == "ST" else "work"
                            for read in holder[ring, w]:
                                pe.wait_ge(*read)
                            name = BANK_READ[step.kind]
                            holder[ring, w] = [(g[name], up(name, step) + k + 1)]
                            return st[:, w, :] if ring == "st" else work[:, w, :]

                        for step in part.steps:
                            kind, m, kb = step.kind, step.m, step.kb
                            par, c = (m // 4) % 2, m % 4
                            wq_, wk_, wv_ = (w2q_sb, w2k_sb, w2v_sb) if step.two else (wq_sb, wk_sb, wqv_sb)
                            if kind == "S":
                                if step.use == 0 and c % 2 == 0:
                                    name = ("qk_load%d" if c == 0 else "qk_late%d") % par
                                    pe.wait_ge(g[name], up(name, step))
                                i, heads, keys = score_uses(causal)[step.use]
                                bank = take(step, 0)
                                for k, h in enumerate(heads):
                                    p = 2 * c + h % 2
                                    o = bank[:, k * keys:(k + 1) * keys]
                                    mm = nc.tensor.matmul(o, qpad[0:MAX_ROW, par, c, h, i * 128:(i + 1) * 128],
                                                          kk[0:MAX_ROW, par, p * S:p * S + keys], start=True,
                                                          stop=not causal)
                                    if causal:
                                        mm = nc.tensor.matmul(o[:, keys - 128:keys], id16[:], tri_sb[:],
                                                              start=False, stop=True)
                                mm.then_inc(g["s_ready"], 1)
                            elif kind == "mT":
                                bank = take(step, 0).bitcast(BF16)
                                pe.wait_ge(g["split"], up("split", step))
                                for i in range(NB):
                                    mm = nc.tensor.transpose(bank[0:12, i * 128:(i + 1) * 128], nms[:, m % 2, i, :], id16[:])
                                mm.then_inc(g["mT_psum"], 1)
                            elif kind == "ST":
                                if kb == 0 and step.use == 0:
                                    name = "max_row%d" % (m % 2)
                                    pe.wait_ge(g[name], up(name, step))
                                heads, queries = exp_uses(causal, kb)[step.use]
                                bank = take(step, 0)
                                for a, h in enumerate(heads):
                                    p = 2 * c + h % 2
                                    mm = nc.tensor.matmul(bank[:, a * queries:(a + 1) * queries],
                                                          kk[0:ROWS, par, p * S + kb * 128:p * S + (kb + 1) * 128],
                                                          qpad[0:ROWS, par, c, h, S - queries:S], start=True, stop=True)
                                mm.then_inc(g["st_ready"], 1)
                            elif kind == "PV":
                                made = part.by["ST", m, kb] if m >= 0 else None
                                if kb == 0:
                                    pe.wait_ge(g["pv_read"], up("pv_read", step))
                                    if c == 0:
                                        name = "v_ready%d" % par
                                        pe.wait_ge(g[name], up(name, step))
                                if causal:
                                    pe.wait_ge(g["tri_done"], thru("tri_done", made) if made
                                               else up("tri_done", part.steps[0]))
                                pe.wait_ge(g["exp_done"], thru("exp_done", made) if made else up("exp_done", part.steps[0]))
                                lo = kb * 128 if causal else 0
                                for h in range(4):
                                    mm = nc.tensor.matmul(pv[32 * h:32 * h + VW, lo:S], vpad[:, par, kb, 4 * c + h, :],
                                                          E[:, kb, h, 0:S - lo], start=(kb == 0), stop=(kb == NB - 1),
                                                          tile_position=(0, 32 * h), skip_group_check=True)
                                mm.then_inc(g["pv_done"], 1)
                            elif kind == "OT":
                                bank = take(step, 0)
                                pe.wait_ge(g["pv_read"], up("pv_read", step))
                                for i in range(NB):
                                    mm = nc.tensor.transpose(bank[:, i * 128:(i + 1) * 128],
                                                             oT[:, m % 2, i * 128:(i + 1) * 128], id32[:])
                                mm.then_inc(g["oT_psum"], 1)
                            elif kind == "oT":
                                bank = take(step, 0)
                                pe.wait_ge(g["o_done"], up("o_done", step))
                                if not causal:
                                    pe.wait_ge(g["reg_step"], up("reg_step", step))
                                for j in range(NB):
                                    mm = nc.tensor.transpose(bank[:, j * 128:(j + 1) * 128], o_turn[:, step.batch % 2, j, :],
                                                             id32[:])
                                mm.then_inc(g["post_psum"], 1)
                            elif kind == "y":
                                bank = take(step, 0)
                                pe.wait_ge(g["post_read"], up("post_read", step))
                                for j in range(NB):
                                    mm = nc.tensor.matmul(bank[:, j * 128:(j + 1) * 128], oT2[:, j * 128:(j + 1) * 128],
                                                          post_w[:], start=True, stop=True)
                                mm.then_inc(g["y_psum"], 1)
                            elif kind == "xT":
                                bank = take(step, 0)
                                pe.wait_ge(g["xn_ready"], up("xn_ready", step))
                                for j in range(NB):
                                    mm = nc.tensor.transpose(bank[:, j * 128:(j + 1) * 128], xn[:, j, :], id32[:])
                                mm.then_inc(g["xT_psum"], 1)
                            elif kind in ("q", "k"):
                                bank = take(step, 0)
                                pe.wait_ge(g["xT_ready"], up("xT_ready", step))
                                nc.tensor.matmul(bank, (wq_ if kind == "q" else wk_)[:], xT[:], start=True, stop=True
                                                 ).then_inc(g["qk_psum"], 1)
                            elif kind == "tok":
                                for k in range(1 + step.two):
                                    bank = take(step, k)
                                    pe.wait_ge(g["xT_ready"], up("xT_ready", step))
                                    for j in range(NB):
                                        mm = nc.tensor.matmul(bank[:, j * 128:(j + 1) * 128], xT[:, j * 128:(j + 1) * 128],
                                                              wv_[:, k * D:(k + 1) * D], start=True, stop=True)
                                    mm.then_inc(g["tok_psum"], 1)
                            elif kind == "sx":
                                bank = take(step, 0)
                                pe.wait_ge(g["qbd_ready"], up("qbd_ready", step))
                                pe.wait_ge(g["qk_read"], up("qk_read", step))
                                nc.tensor.matmul(bank[0:XQ, :], qbd[:].rearrange("p h r -> p (h r)"), kf[:],
                                                 start=True, stop=True).then_inc(g["sx_psum"], 1)
                            elif kind == "n_eT":
                                bank = take(step, 0)
                                pe.wait_ge(g["n_exp"], up("n_exp", step))
                                for k in range(NB):
                                    mm = nc.tensor.transpose(bank[:, k * XQ:(k + 1) * XQ], ext[:, k * 128:(k + 1) * 128],
                                                             id32[0:XQ, 0:XQ])
                                mm.then_inc(g["n_eT_psum"], 1)
                            elif kind == "n_o":
                                par = step.batch % 2
                                bank = take(step, 0)
                                pe.wait_ge(g["n_eT_read"], up("n_eT_read", step))
                                pe.wait_ge(g["v_ready%d" % par], up("v_ready%d" % par, step))
                                for k in range(NB):
                                    mm = nc.tensor.matmul(bank[0:XQ, 0:D], eT[:, k * XQ:(k + 1) * XQ],
                                                          vpad[:, par, k, :, 0:HD], start=(k == 0), stop=(k == NB - 1))
                                mm.then_inc(g["n_o_psum"], 1)
                            elif kind == "n_sum":
                                bank = take(step, 0)
                                pe.wait_ge(g["n_o_read"], up("n_o_read", step))
                                nc.tensor.matmul(bank[0:REG, 0:D], selr_sb, w80[:], start=True, stop=True
                                                 ).then_inc(g["n_sum_psum"], 1)

                    go(pe, part_work)
                    if causal:
                        pe.wait_ge(g["pv_read"], START + after.after()["pv_read"])
                        class_rows_tensor(pe)

                @block.scalar
                def _(act):
                    def part_work(part):
                        up, thru = part.upto, part.through
                        for step in part.steps:
                            kind, m, kb = step.kind, step.m, step.kb
                            banks = part.banks[step.n]
                            batch = 2 * part.turn + step.batch
                            if kind == "ST":
                                heads, queries = exp_uses(causal, kb)[step.use]
                                if step.use == 0:
                                    act.wait_ge(g["pv_done"], up("pv_done", step) - 2)
                                act.wait_ge(g["st_ready"], thru("st_ready", step))
                                src = st[:, banks[0], 0:queries * len(heads)].rearrange("p (h q) -> p h q", q=queries)
                                nc.scalar.activation(E[:, kb, heads[0]:heads[-1] + 1, 0:queries],
                                                     src, ACT.Exp, scale=SCALE
                                                     ).then_inc(g["exp_done"], 1)
                            elif kind == "PV" and kb == 3:
                                act.wait_ge(g["pv_done"], thru("pv_done", step))
                                act.wait_ge(g["oT_psum"], up("oT_psum", step))
                                nc.scalar.copy(oT[:, m % 2, :], pv[:]).then_inc(g["pv_read"], 1)
                            elif kind == "mT":
                                act.wait_ge(g["mT_psum"], thru("mT_psum", step))
                                name = "max_row%d" % (m % 2)
                                act.wait_ge(g[name], up(name, step))
                                nc.scalar.copy(mT[:, m % 2, :], work[:, banks[0], :].bitcast(BF16)[0:12, 0:512]
                                               ).then_inc(g["mT_ready"], 1)
                            elif kind == "oT":
                                act.wait_ge(g["post_psum"], thru("post_psum", step))
                                act.wait_ge(g["y_psum"], up("y_psum", step))
                                nc.scalar.copy(oT2[:], work[:, banks[0], :]).then_inc(g["post_read"], 1)
                            elif kind == "xT":
                                act.wait_ge(g["xT_psum"], thru("xT_psum", step))
                                act.wait_ge(g["tok_psum"], up("tok_psum", step))
                                nc.scalar.copy(xT[:], work[:, banks[0], :]).then_inc(g["xT_ready"], 1)
                            elif kind in ("q", "k"):
                                s = 0 if kind == "q" else 1
                                dst, bias = ((qf, bq_sb), (kf, bk_sb))[s]
                                act.wait_ge(g["qk_psum"], thru("qk_psum", step))
                                act.wait_ge(g["part_done%d" % s], up("part_done%d" % s, step))
                                act.wait_ge(g["qbd_ready"], up("qbd_ready", step))
                                act.wait_ge(g["sx_psum"], up("sx_psum", step))
                                if step.two:
                                    ins = nc.scalar.copy(dst[:], work[:, banks[0], :])
                                else:
                                    ins = nc.scalar.activation(dst[:], work[:, banks[0], :], ACT.Identity, bias=bias[:])
                                ins.then_inc(g["qk_read"], 1)
                                act.wait_ge(g["stored%d" % s], up("stored%d" % s, step))
                                act.wait_ge(g["qk_read"], up("qk_read", step) + 1)
                                nc.scalar.copy(parts[:, s, 1, :], dst[:]).then_inc(g["qk_read"], 1)
                            elif kind in ("split1", "split4"):
                                s = int(kind[5:]) // 3
                                name = "part_done%d" % s
                                act.wait_ge(g[name], up(name, step))
                                nc.scalar.copy(parts[:, s, 0, :], res[:, s, :]).then_inc(g[name], 1)
                            elif kind == "tok" and step.two:
                                act.wait_ge(g["tok_psum"], up("tok_psum", step) + 1)
                                w3 = work[:, banks[0], :].rearrange("p (j d) -> p j d", d=D)
                                nc.scalar.copy(v_all[:, batch, :, :], w3).then_inc(g["tok_read"], 1)
                                act.wait_ge(g["tok_psum"], up("tok_psum", step) + 2)
                                act.wait_ge(g["sim_pool"], up("sim_pool", step))
                                nc.scalar.copy(qtok[:], work[:, banks[1], :]).then_inc(g["tok_read"], 1)
                            elif kind == "n_exp":
                                act.wait_ge(g["n_step"], up("n_step", step))
                                act.wait_ge(g["n_o_read"], up("n_o_read", step))
                                nc.scalar.activation(ext[:], ext[:], ACT.Exp, scale=SCALE, bias=xm[:], accum_out=xsum[:]
                                                     ).then_inc(g["n_exp"], 1)
                            elif kind == "sx":
                                act.wait_ge(g["sx_psum"], thru("sx_psum", step))
                                nc.scalar.copy(sx_all[:, batch, :], work[0:XQ, banks[0], :]).then_inc(g["sx_read"], 1)

                    go(act, part_work)

                @block.vector
                def _(dve):
                    def statistics(steps, src, half):
                        blocks = range(half * NB // 2, (half + 1) * NB // 2)
                        for j in blocks:
                            steps.done(nc.vector.bn_stats(stats[:, j, :], src[:, j, :]))
                        steps.settle()
                        apart(dve)
                        for j in blocks:
                            steps.done(nc.vector.bn_aggr(mv[:, j, :], stats[:, j, :]))
                        if half:
                            steps.settle()
                            steps.done(nc.vector.tensor_scalar(rstd[:], mv[:, :, 1], EPS, None, ALU.add))

                    def part_work(part):
                        up, thru = part.upto, part.through
                        for step in part.steps:
                            kind, m, kb = step.kind, step.m, step.kb
                            banks = part.banks[step.n]
                            batch = 2 * part.turn + step.batch
                            par, c = (m // 4) % 2, m % 4
                            if kind == "S":
                                if step.use == 0:
                                    dve.wait_ge(g["split"], up("split", step) - 1)
                                i, heads, keys = score_uses(causal)[step.use]
                                dve.wait_ge(g["s_ready"], thru("s_ready", step))
                                src = work[:, banks[0], 0:keys * len(heads)].rearrange("p (h k) -> p h k", k=keys)
                                nc.vector.tensor_reduce(nm[:, m % 2, i, heads[0]:heads[-1] + 1], src, AX.X, ALU.max,
                                                        negate=True).then_inc(g["max_done"], 1)
                            elif kind == "OT":
                                o4 = work[:, banks[0], :].rearrange("p (i g r) -> p i g r", i=NB, g=4)
                                dve.wait_ge(g["oT_psum"], thru("oT_psum", step))
                                dve.wait_ge(g["o_done"], up("o_done", step))
                                nc.vector.reciprocal(rec[:], o4[:, :, :, HD]).then_inc(g["rec_done"], 1)
                                dve.wait_ge(g["rec_done"], thru("rec_done", step))
                                dve.wait_ge(g["post_psum"], up("post_psum", step))
                                dst = o_turn[:, par, :, 4 * HD * c:4 * HD * (c + 1)].rearrange("p i (g d) -> p i g d", d=HD)
                                nc.vector.tensor_tensor(dst, o4[:, :, :, 0:HD],
                                                        rec[:].unsqueeze(3).to_broadcast([128, NB, 4, HD]),
                                                        ALU.mult).then_inc(g["o_done"], 1)
                            elif kind == "n_add":
                                par = step.batch % 2
                                dve.wait_ge(g["qk_late%d" % par], up("qk_late%d" % par, step))
                                dve.wait_ge(g["n_eT_psum"], up("n_eT_psum", step))
                                apart(dve)
                                nc.vector.tensor_tensor(ext[:], sx_all[:, batch, :], pen[:, par, :], ALU.add
                                                        ).then_inc(g["n_step"], 1)
                            elif kind == "n_max":
                                steps = Steps(dve, g["n_step"], up("n_step", step))
                                steps.settle()
                                dve.wait_ge(g["n_exp"], up("n_exp", step))
                                apart(dve)
                                steps.done(nc.vector.tensor_reduce(xm[:], ext[:], AX.X, ALU.max, negate=True))
                                steps.settle()
                                steps.done(nc.vector.tensor_scalar(xm[:], xm[:], SCALE, None, ALU.mult))
                            elif kind == "n_eT":
                                dve.wait_ge(g["n_eT_psum"], thru("n_eT_psum", step))
                                dve.wait_ge(g["n_o_psum"], up("n_o_psum", step))
                                nc.vector.tensor_copy(eT[:], work[:, banks[0], 0:NB * XQ]).then_inc(g["n_eT_read"], 1)
                                nc.vector.reciprocal(xsum[:], xsum[:]).then_inc(g["n_step"], 1)
                            elif kind == "n_o":
                                dve.wait_ge(g["n_step"], up("n_step", step))
                                dve.wait_ge(g["n_sum_psum"], up("n_sum_psum", step))
                                dve.wait_ge(g["n_o_psum"], thru("n_o_psum", step))
                                nc.vector.scalar_tensor_tensor(out=w80[:], in0=work[0:XQ, banks[0], 0:D], scalar=xsum[:],
                                                               in1=bd_c, op0=ALU.mult, op1=ALU.mult
                                                               ).then_inc(g["n_o_read"], 1)
                            elif kind == "n_sum":
                                dve.wait_ge(g["reg_step"], up("reg_step", step))
                                dve.wait_ge(g["n_sum_psum"], thru("n_sum_psum", step))
                                nc.vector.tensor_copy(o_neg[:, step.batch % 2, :], work[0:REG, banks[0], 0:D]
                                                      ).then_inc(g["n_sum_read"], 1)
                            elif kind == "reg" and not causal:
                                o = o_turn[0:REG, step.batch % 2, 0, :]
                                dve.wait_ge(g["o_done"], up("o_done", step))
                                dve.wait_ge(g["n_sum_read"], up("n_sum_read", step))
                                nc.vector.tensor_tensor(o, o, o_neg[:, step.batch % 2, :], ALU.add).then_inc(g["reg_step"], 1)
                                dve.wait_ge(g["reg_step"], up("reg_step", step) + 1)
                                nc.vector.tensor_scalar(o, o, 0.5, None, ALU.mult).then_inc(g["reg_step"], 1)
                            elif kind == "y":
                                dve.wait_ge(g["x_done"], up("x_done", step))
                                dve.wait_ge(g["y_psum"], thru("y_psum", step))
                                nc.vector.tensor_tensor(y_sb[:], work[:, banks[0], :].rearrange("p (j d) -> p j d", d=D),
                                                        post_b[:].unsqueeze(1).to_broadcast([128, NB, D]),
                                                        ALU.add).then_inc(g["y_read"], 1)
                            elif kind.startswith(("y_stats", "xn_stats")):
                                steps = Steps(dve, g["dve_step"], up("dve_step", step))
                                steps.settle()
                                dve.wait_ge(g["x_done"], up("x_done", step))
                                dve.wait_ge(g["xn_ready"], up("xn_ready", step))
                                dve.wait_ge(g["y_read"], up("y_read", step))
                                apart(dve)
                                statistics(steps, y_sb if kind[0] == "y" else x_all[:, batch, :, :], int(kind[-1]))
                            elif kind.startswith("x_new") and (causal or part is after):
                                steps = Steps(dve, g["dve_step"], up("dve_step", step))
                                steps.settle()
                                dve.wait_ge(g["pow_done"], up("pow_done", step))
                                half = int(kind[-1])
                                for j in range(half * NB // 2, (half + 1) * NB // 2):
                                    steps.done(nc.vector.tensor_scalar(y_sb[:, j, :], y_sb[:, j, :], mv[:, j, 0:1],
                                                                       rstd[:, j:j + 1], ALU.subtract, ALU.mult))
                                if half:
                                    steps.settle()
                                    nc.vector.tensor_tensor(x_all[:, batch, :, :], x_all[:, batch, :, :], y_sb[:],
                                                            ALU.add).then_inc(g["x_done"], 1)
                            elif kind in ("xn0", "xn1"):
                                dve.wait_ge(g["xT_psum"], up("xT_psum", step))
                                dve.wait_ge(g["pow_done"], up("pow_done", step))
                                half = int(kind[-1])
                                for j in range(half * NB // 2, (half + 1) * NB // 2):
                                    nc.vector.tensor_scalar(xn[:, j, :], x_all[:, batch, j, :], mv[:, j, 0:1], rstd[:, j:j + 1],
                                                            ALU.subtract, ALU.mult).then_inc(g["xn_ready"], 1)
                            elif kind == "tok" and not step.two:
                                dve.wait_ge(g["tok_psum"], thru("tok_psum", step))
                                w3 = work[:, banks[0], :].rearrange("p (j d) -> p j d", d=D)
                                nc.vector.tensor_tensor(v_all[:, batch, :, :], w3,
                                                        bv_bc[:].unsqueeze(1).to_broadcast([128, NB, D]), ALU.add).then_inc(g["tok_read"], 1)
                            elif kind == "qbd":
                                dve.wait_ge(g["qk_read"], up("qk_read", step))
                                dve.wait_ge(g["sx_psum"], up("sx_psum", step))
                                nc.vector.tensor_tensor(qbd[:], bd_r[:], qf[:, 0:REG].unsqueeze(1).to_broadcast([128, H, REG]),
                                                        ALU.mult).then_inc(g["qbd_ready"], 1)
                            elif kind == "sim_qq" and part is after and step.batch == 1:
                                dve.wait_ge(g["tok_read"], up("tok_read", step))
                                dve.wait_ge(g["sim_dve"], up("sim_dve", step))
                                nc.vector.tensor_tensor(prod[:, 1, :], qtok[:], qtok[:], ALU.mult).then_inc(g["sim_pool"], 1)
                            elif kind == "sim_sums":
                                dve.wait_ge(g["sim_dve"], up("sim_dve", step))
                                dve.wait_ge(g["sim_pool"], up("sim_pool", step))
                                for k, dst in enumerate((dots, nrm2)):
                                    nc.vector.tensor_reduce(dst[:], prod[:, k, :].rearrange("p (a d) -> p a d", d=HD),
                                                            AX.X, ALU.add).then_inc(g["sim_dve"], 1)
                            elif kind.startswith("sim_root"):
                                steps = Steps(dve, g["sim_dve"], up("sim_dve", step))
                                steps.settle()
                                if kind == "sim_root0":
                                    steps.done(nc.vector.tensor_scalar(rs[:].bitcast(I32), nrm2[:].bitcast(I32), -0.5,
                                                                       RSQRT_BITS, ALU.mult, ALU.add))
                                    steps.settle()
                                steps.done(nc.vector.tensor_tensor(rs2[:], rs[:], rs[:], ALU.mult))
                                steps.settle()
                                steps.done(nc.vector.scalar_tensor_tensor(rs2[:], rs2[:], -0.5, nrm2[:], ALU.mult, ALU.mult))
                                steps.settle()
                                steps.done(nc.vector.scalar_tensor_tensor(rs[:], rs2[:], 1.5, rs[:], ALU.add, ALU.mult))
                                if kind == "sim_root2":
                                    steps.settle()
                                    steps.done(nc.vector.tensor_tensor(dots[:], dots[:], rs[:], ALU.mult))
                                    steps.settle()
                                    apart(dve)
                                    steps.done(nc.vector.tensor_reduce(sim[:, batch, :],
                                                                       dots[:].rearrange("p (j h) -> p j h", h=H),
                                                                       AX.X, ALU.add))

                    def group_norms():
                        nc.vector.tensor_tensor(prod[:, 0, 0:D], g_bc, g_bc, ALU.mult).then_inc(g_step, 1)
                        dve.wait_ge(g_step, 1)
                        nc.vector.tensor_reduce(g_n[:], prod[:, 0, 0:D].rearrange("p (h d) -> p h d", d=HD),
                                                AX.X, ALU.add).then_inc(g_step, 1)

                    go(dve, part_work, group_norms)
                    if causal:
                        class_rows_vector(dve)

                @block.gpsimd
                def _(pool):
                    def raise_half(t, name):
                        nc.gpsimd.tensor_tensor(t[:], t[:], mhalf[:, 0:t.shape[1]], ALU.pow).then_inc(g[name], 1)

                    def part_work(part):
                        up, thru = part.upto, part.through
                        for step in part.steps:
                            kind, m, kb = step.kind, step.m, step.kb
                            batch = 2 * part.turn + step.batch
                            if kind == "ST" and counts(step, causal)["tri_done"]:
                                pool.wait_ge(g["exp_done"], thru("exp_done", step))
                                apart(pool)
                                diag = E[:, kb, :, 0:128]
                                nc.gpsimd.affine_select(out=diag, in_=diag, compare_op=ALU.is_ge, fill=0.0, base=0,
                                                        pattern=[[0, 4], [1, 128]], channel_multiplier=-1
                                                        ).then_inc(g["tri_done"], 1)
                            elif kind == "S" and counts(step, causal)["split"]:
                                steps = Steps(pool, g["split_step"], up("split_step", step))
                                pool.wait_ge(g["max_done"], thru("max_done", step))
                                pool.wait_ge(g["mT_psum"], up("mT_psum", step) - 1)
                                apart(pool)
                                n4, r4 = nm[:, m % 2], nmr[:, m % 2]
                                part3 = [nms[:, m % 2, :, 4 * t:4 * t + 4] for t in range(3)]
                                steps.done(nc.gpsimd.tensor_copy(part3[0], n4))
                                steps.settle()
                                steps.done(nc.gpsimd.tensor_tensor(r4, n4, part3[0], ALU.subtract))
                                steps.settle()
                                apart(pool)
                                steps.done(nc.gpsimd.tensor_copy(part3[1], r4))
                                steps.settle()
                                steps.done(nc.gpsimd.tensor_tensor(r4, r4, part3[1], ALU.subtract))
                                steps.settle()
                                apart(pool)
                                nc.gpsimd.tensor_copy(part3[2], r4).then_inc(g["split"], 1)
                            elif kind == "lay":
                                par = step.batch % 2
                                pool.wait_ge(g["pv_done"], up("pv_done", step))
                                pool.wait_ge(g["n_o_psum"], up("n_o_psum", step))
                                pool.wait_ge(g["tok_read"], up("tok_read", step))
                                apart(pool)
                                nc.gpsimd.tensor_copy(vpad[:, par, :, :, 0:HD].rearrange("p k h d -> p (k h) d"),
                                                      v_all[:, batch, :, :].rearrange("p k (h d) -> p (k h) d", d=HD)
                                                      ).then_inc(g["v_ready%d" % par], 1)
                            elif kind in ("y_stats1", "xn_stats1"):
                                pool.wait_ge(g["dve_step"], thru("dve_step", step))
                                raise_half(rstd, "pow_done")
                            elif kind.startswith("x_new") and not causal and part is not after:
                                steps = Steps(pool, g["dve_step"], up("dve_step", step))
                                steps.settle()
                                pool.wait_ge(g["y_read"], up("y_read", step))
                                pool.wait_ge(g["pow_done"], up("pow_done", step))
                                apart(pool)
                                half = int(kind[-1])
                                for j in range(half * NB // 2, (half + 1) * NB // 2):
                                    steps.done(nc.gpsimd.tensor_scalar(y_sb[:, j, :], y_sb[:, j, :], mv[:, j, 0:1],
                                                                       rstd[:, j:j + 1], ALU.subtract, ALU.mult))
                                if half:
                                    steps.settle()
                                    nc.gpsimd.tensor_tensor(x_all[:, batch, :, :], x_all[:, batch, :, :], y_sb[:],
                                                            ALU.add).then_inc(g["x_done"], 1)
                            elif kind in ("split0", "split2", "split3", "split5"):
                                k, n = divmod(int(kind[5:]), 3)
                                src = (qf, kf)[k]
                                pool.wait_ge(g["qk_read"], up("qk_read", step))
                                name = "part_done%d" % k
                                pool.wait_ge(g[name], up(name, step))
                                if n == 0:
                                    nc.gpsimd.tensor_tensor(res[:, k, :], src[:], parts[:, k, 1, :], ALU.subtract
                                                            ).then_inc(g[name], 1)
                                else:
                                    nc.gpsimd.tensor_tensor(parts[:, k, 2, :], res[:, k, :], parts[:, k, 0, :], ALU.subtract
                                                            ).then_inc(g[name], 1)
                            elif kind in ("sim_qg", "sim_qq"):
                                pool.wait_ge(g["tok_read"], up("tok_read", step))
                                pool.wait_ge(g["sim_dve"], up("sim_dve", step))
                                if kind == "sim_qg":
                                    ins = nc.gpsimd.tensor_tensor(prod[:, 0, :].rearrange("p (j d) -> p j d", d=D),
                                                                  qtok[:].rearrange("p (j d) -> p j d", d=D),
                                                                  g_bc[:].unsqueeze(1).to_broadcast([128, NB, D]), ALU.mult)
                                    ins.then_inc(g["sim_pool"], 1)
                                elif not (part is after and step.batch == 1):
                                    nc.gpsimd.tensor_tensor(prod[:, 1, :], qtok[:], qtok[:], ALU.mult
                                                            ).then_inc(g["sim_pool"], 1)

                    def group_scaled():
                        pool.wait_ge(halves, 1)
                        pool.wait_ge(g_step, 2)
                        nc.gpsimd.tensor_tensor(g_n[:], g_n[:], mhalf[:, 0:H], ALU.pow).then_inc(g_step, 1)
                        pool.wait_ge(g_step, 3)
                        g3 = g_bc.rearrange("p (h d) -> p h d", d=HD)
                        nc.gpsimd.tensor_tensor(g3, g3, g_n[:].unsqueeze(2).to_broadcast([128, H, HD]), ALU.mult
                                                ).then_inc(g_step, 1)
                        pool.wait_ge(g_step, 4)

                    if causal:
                        class_rows_first(pool)
                    go(pool, part_work, group_scaled)
                    if causal:
                        class_rows_gpsimd(pool)

                @block.sync
                def _(sp):
                    def part_work(part):
                        up, thru = part.upto, part.through
                        for step in part.steps:
                            kind, m = step.kind, step.m
                            batch = 2 * part.turn + step.batch
                            if kind == "load":
                                par = step.batch % 2
                                there = g["qk_load%d" % par]
                                sp.wait_ge(g["st_ready"], up("st_ready", step))
                                apart(sp)
                                if causal:
                                    for name in ("stored0", "stored1"):
                                        sp.wait_ge(g[name], up(name, step))
                                        apart(sp)
                                early = not causal and part is ahead
                                if not early:
                                    load_rows(sp, causal, batch, par, 0, there)
                                if not causal:
                                    sp.wait_ge(g["n_step"], up("n_step", step))
                                    apart(sp)
                                    sp.dma_start(qpad[96:98, par].rearrange("r c g s -> r (c g) s"),
                                                 m_scr[0:2, batch, :].unsqueeze(1).to_broadcast([2, H, S])).then_inc(there, 16)
                                    sp.dma_start(kk[96:98, par].rearrange("r (p s) -> r p s", s=S),
                                                 m_scr[2:4, batch, :].unsqueeze(1).to_broadcast([2, PAIRS, S])).then_inc(there, 16)
                                    sp.dma_start(pen[:, par, :], m_scr[4:5, batch, :].to_broadcast([XQ, S])
                                                 ).then_inc(g["qk_late%d" % par], 16)
                                if not early:
                                    load_rows(sp, causal, batch, par, 1, g["qk_late%d" % par])
                            elif kind == "OT" and causal and part is after:
                                sp.wait_ge(g["st_ready"], up("st_ready", step))
                                for name in ("stored0", "stored1"):
                                    sp.wait_ge(g[name], START + last.start[name])
                                apart(sp)
                                load_rows(sp, False, 0, 0, 0, signal["p2_qk_load0"])
                                load_rows(sp, False, 0, 0, 1, signal["p2_qk_late0"])
                            elif kind == "mT":
                                sp.wait_ge(g["mT_ready"], thru("mT_ready", step))
                                apart(sp)
                                sp.dma_start(qpad[MAX_ROW:ROWS, (m // 4) % 2, m % 4], mT[:, m % 2, :]
                                             ).then_inc(g["max_row%d" % (m % 2)], 16)
                            elif kind.startswith("split"):
                                s, n = divmod(int(kind[5:]), 3)
                                p = STORED_AT[n]
                                if n == 0:
                                    sp.wait_ge(g["qk_read"], up("qk_read", step))
                                else:
                                    name = "part_done%d" % s
                                    sp.wait_ge(g[name], thru(name, step))
                                apart(sp)
                                for t in TERMS_OF[s][p]:
                                    sp.dma_start((q_scr, k_scr)[s][not step.two][batch, :, t, :, :], parts[:, s, p, :]
                                                 ).then_inc(g["stored%d" % s], 16)
                            elif kind == "x_new1" and not causal:
                                sp.wait_ge(g["x_done"], thru("x_done", step))
                                apart(sp)
                                sp.dma_start(out[batch].rearrange("(j p) d -> p j d", p=128), x_all[:, batch, :, :]
                                             ).then_inc(g["out_done"], 16)

                    go(sp, part_work)
                    if causal:
                        class_rows_sync(sp)
                    for name in ("stored0", "stored1", "out_done"):
                        if after.after()[name]:
                            sp.wait_ge(g[name], START + after.after()[name])

        phase("p1_", True)
        phase("p2_", False)


def kernel(**inputs):
    import ml_dtypes
    import numpy as np
    import concourse.bacc as bacc
    from concourse.bass_utils import run_bass_kernel_spmd as run

    a = {k: np.asarray(v) for k, v in inputs.items()}

    def pair_rows(w):
        return w.reshape((4, 2, 2, HD) + w.shape[1:]).transpose((1, 3, 0, 2) + tuple(range(4, 3 + w.ndim))).reshape(w.shape)

    w2 = a["L0_ffn_W_qkv"]
    head = pair_rows(np.repeat(np.arange(H), HD))
    cols = np.repeat(np.arange(H), REG)
    side = np.concatenate
    arrays = {
        "x": a["L0_attn_x"],
        "near": side([pair_rows(a["L0_attn_Wq"]).T, pair_rows(a["L0_attn_Wk"]).T, a["L0_attn_Wv"].T,
                      np.eye(128, dtype=np.float32), pair_rows(a["L0_attn_bq"])[:, None],
                      pair_rows(a["L0_attn_bk"])[:, None]], axis=1),
        "rows": side([a["L0_attn_bv"], a["L0_attn_bo"], a["L0_ffn_b_proj"], a["L0_ffn_g_info"][0, 0]])[None, :],
        "tri": np.triu(np.full((128, 128), -BIG, dtype=np.float32), 1).astype(ml_dtypes.bfloat16),
        "far": side([a["L0_attn_Wo"].T, pair_rows(w2[:, 0:D].T).T, pair_rows(w2[:, D:2 * D].T).T, w2[:, 2 * D:3 * D],
                     w2[:, 0:D], a["L0_ffn_W_proj"], (head[:, None] == cols[None, :]).astype(np.float32)], axis=1),
        "reg_tables": side([(cols[:, None] == np.repeat(np.arange(H), HD)[None, :]).astype(np.float32),
                            (np.tile(np.arange(REG), H)[:, None] == np.arange(REG)[None, :]).astype(np.float32)], axis=1),
    }
    arrays = {k: np.ascontiguousarray(v) for k, v in arrays.items()}
    nc = bacc.Bacc("TRN2", target_bir_lowering=False, num_devices=1)
    aps = {k: nc.dram_tensor(k, v.shape, mybir.dt.from_np(v.dtype), kind="ExternalInput").ap() for k, v in arrays.items()}
    out = nc.dram_tensor("out", (B, S, D), F32, kind="ExternalOutput").ap()
    build(nc, out=out, **aps)
    r = run(nc, [arrays], core_ids=[0])
    return r.results[0]["out"]
```
